# Optimizing a Trainium2 kernel written in Bass

```python
import numpy as np
import jax
import jax.numpy as jnp

def _softmax(x, axis=-1):
    return jax.nn.softmax(x, axis=axis)

def _gelu(x):
    return jax.nn.gelu(x, approximate=True)

def _silu(x):
    return jax.nn.silu(x)

def _sigmoid(x):
    return jax.nn.sigmoid(x)

def _layernorm(x, axis=-1, eps=1e-05):
    m = jnp.mean(x, axis=axis, keepdims=True)
    v = jnp.var(x, axis=axis, keepdims=True)
    return (x - m) / jnp.sqrt(v + eps)

def _scatter_add(tgt, idx, src, axis=0):
    return tgt.at[idx].add(src)

def _segment_sum(src, seg, n):
    return jax.ops.segment_sum(src, seg, n)
kernel_name = 'mk_flamingo_gated_d1_seqx_r4_f7bd2b'

def setup_inputs(seed: int=0):
    np.random.seed(seed)
    _w = jnp.asarray

    def _rec_inputs():
        import jax
        import jax.numpy as jnp
        _rk = jax.random.key(seed)
        x = 7.22e-05 + 1 * jax.random.normal(jax.random.fold_in(_rk, 1), (8, 256, 512), jnp.float32)
        _lenS = 256 - jax.random.randint(jax.random.fold_in(_rk, 7), (8,), 0, max(1, 256 // 4) + 1, jnp.int32)
        _lenS2 = 256 - jax.random.randint(jax.random.fold_in(_rk, 8), (8,), 0, max(1, 256 // 4) + 1, jnp.int32)
        _ctx_2048P = jax.random.normal(jax.random.fold_in(_rk, 11), (8, 16, 512), jnp.float32)
        _ctx_2048c = jax.random.dirichlet(jax.random.fold_in(_rk, 511), 0.3 * jnp.ones((16,), jnp.float32), (8, 256))
        _ctx_2048t = jnp.einsum('bsk,bkd->bsd', _ctx_2048c, _ctx_2048P)
        _ctx_2048t = _ctx_2048t * jax.lax.rsqrt(jnp.mean(jnp.square(_ctx_2048t)) + 1e-12) * 0.953939
        ctx_2048 = 4.13588e-05 + 0.999923 * (_ctx_2048t + 0.3 * jax.random.normal(jax.random.fold_in(_rk, 611), (8, 256, 512), jnp.float32))
        _g = jax.random.normal(jax.random.fold_in(_rk, 9001), (2, 1), jnp.float32)
        _g = jnp.sign(_g) * jnp.maximum(jnp.abs(_g), 1.0) + (_g == 0) * 1.0
        g_xattn = _g[0]
        g_ffn = _g[1]
        return (x, ctx_2048, g_xattn, g_ffn)
    x, ctx_2048, g_xattn, g_ffn = _rec_inputs()

    def _L0_xattn_setup():
        import jax, jax.numpy as jnp
        import numpy as np
        N_HEAD = 8
        key = jax.random.key(seed)
        k1, k2, k3 = jax.random.split(key, 3)
        B, D, L = (4, 256, 512)
        q = jax.random.normal(k1, (B, D, L), dtype=jnp.float32)
        k = jax.random.normal(k2, (B, D, L), dtype=jnp.float32)
        v = jax.random.normal(k3, (B, D, L), dtype=jnp.float32)
        gamma = jnp.ones((), dtype=jnp.float32)
        return {'q': q, 'k': k, 'v': v, 'gamma': gamma}
    _L0_xattn_all = _L0_xattn_setup()
    _L0_xattn_in = {k: v for k, v in _L0_xattn_all.items() if k in ('gamma',)}
    del _L0_xattn_all

    def _L0_ffn_setup():
        import jax, jax.numpy as jnp
        import numpy as np
        FP8 = jnp.float8_e4m3fn
        key = jax.random.key(seed)
        k1, k2 = jax.random.split(key)
        input1 = jax.random.normal(k1, (2, 1024, 512), dtype=jnp.float32)
        input2 = jax.random.normal(k2, (512, 512), dtype=jnp.float32)
        scale = jnp.array(0.5, dtype=jnp.float32)
        scale1 = jnp.array(0.5, dtype=jnp.float32)
        return {'input1': input1, 'input2': input2, 'scale': scale, 'scale1': scale1}
    _L0_ffn_all = _L0_ffn_setup()
    _L0_ffn_in = {k: v for k, v in _L0_ffn_all.items() if k in ('input2', 'scale', 'scale1')}
    del _L0_ffn_all
    return {'x': x, 'ctx_2048': ctx_2048, 'g_xattn': g_xattn, 'g_ffn': g_ffn, 'L0_xattn_gamma': _L0_xattn_in['gamma'], 'L0_ffn_input2': _L0_ffn_in['input2'], 'L0_ffn_scale': _L0_ffn_in['scale'], 'L0_ffn_scale1': _L0_ffn_in['scale1']}

def reference(x, ctx_2048, g_xattn, g_ffn, L0_xattn_gamma, L0_ffn_input2, L0_ffn_scale, L0_ffn_scale1):
    import jax
    import jax.numpy as jnp

    def _L0_xattn_ref(q, k, v, gamma):
        import jax, jax.numpy as jnp
        import numpy as np
        N_HEAD = 8
        B, Dq, Lq = q.shape
        Dv, Lk = (v.shape[-2], v.shape[-1])
        h = N_HEAD
        dq = Dq // h
        dv = Dv // h
        qh = q.reshape(B, h, dq, Lq)
        kh = k.reshape(B, h, dq, Lk)
        vh = v.reshape(B, h, dv, Lk)
        scale = 1.0 / jnp.sqrt(jnp.asarray(dq, dtype=q.dtype))
        qk = jnp.einsum('bhdq,bhdl->bhql', qh, kh) * scale
        sm = jax.nn.softmax(qk, axis=-1)
        ret = jnp.einsum('bhql,bhdl->bhdq', sm, vh)
        ret = ret.reshape(B, Dv, Lq)
        return gamma * ret

    def _L0_ffn_ref(input1, input2, scale, scale1):
        import jax, jax.numpy as jnp
        import numpy as np
        FP8 = jnp.float8_e4m3fn
        q1 = (input1 * scale).astype(FP8)
        q2 = (input2 * scale1).astype(FP8)
        d1 = q1.astype(jnp.float32) * (1.0 / scale)
        d2 = q2.astype(jnp.float32) * (1.0 / scale1)
        return jnp.einsum('bmk,kn->bmn', d1, d2)
    x = x + jnp.tanh(g_xattn[0]) * _L0_xattn_ref(_layernorm(x, axis=-1), ctx_2048, ctx_2048, L0_xattn_gamma)
    x = x + jnp.tanh(g_ffn[0]) * _L0_ffn_ref(_layernorm(x, axis=-1), L0_ffn_input2, L0_ffn_scale, L0_ffn_scale1)
    return x

_drawn_inputs = setup_inputs


def setup_inputs(seed=0):
    import zlib

    import numpy as np

    out = dict(_drawn_inputs(seed))
    spreads = {}
    factors = {}
    for name, (base, spread) in spreads.items():
        noise = np.random.default_rng([zlib.crc32(name.encode()), seed]).standard_normal(out[name].shape)
        drawn = base * np.exp(spread * noise) if base else spread * noise
        out[name] = jnp.asarray(drawn.astype(out[name].dtype))
    for name, factor in factors.items():
        out[name] = (out[name] * factor).astype(out[name].dtype)
    return out
```

```python
from contextlib import ExitStack

import concourse.bass as bass
from concourse import mybir

F32 = mybir.dt.float32
F32R = mybir.dt.float32r
BF16 = mybir.dt.bfloat16
U32 = mybir.dt.uint32
ALU = mybir.AluOpType
ACT = mybir.ActivationFunctionType
AX = mybir.AxisListType.X

P = 128
L = 512
D = 32
IMAGES, CHANNELS = 8, 256
TILES = IMAGES * CHANNELS // P
HEADS_PER_TILE = P // D
PAIR = 2
STEPS = TILES * HEADS_PER_TILE // PAIR
CHUNKS = L // P
UNITS = PAIR * CHUNKS
SLOTS = 2 * HEADS_PER_TILE
ONES_ROW = 3 * D
Q_HI, Q_LO, K_HI, K_LO = range(4)
STACKED = ((Q_HI, K_HI), (Q_LO, K_HI), (Q_HI, K_LO))
STACK_DMAS = PAIR * len(STACKED)
LN_EPS = 1e-5
SM_SCALE = float(D) ** -0.5
DMA = 16

EXPONENT_BITS = 0x7F800000
ROUND_AT = 1.5 * 2.0 ** 20
ROUND_LEAST = ROUND_AT * 2.0 ** -6
FP8_MAX = 448.0
HUGE = 3.0e38

FIRST_STEP, LOOP_FIRST, LOOPS, LAST_STEP = -6, 10, 4, STEPS + 10
BODY = 4


def upto(eng, sem, count, i, per_loop):
    if i is None:
        if count > 0:
            eng.wait_ge(sem, count)
    else:
        assert count > 0
        eng.wait_ge(sem, i * per_loop + count)


def runs(index, i, n, per_loop):
    if i is None:
        return 0 <= index < n
    assert index >= 0 and index + per_loop * (LOOPS - 1) < n
    return True


def steps(eng, step):
    for s in range(FIRST_STEP, LOOP_FIRST):
        step(s, None)
    with eng.Fori(0, LOOPS) as i:
        for s in range(LOOP_FIRST, LOOP_FIRST + BODY):
            step(s, i)
    for s in range(LOOP_FIRST + BODY * LOOPS, LAST_STEP):
        step(s, None)


def build(nc, x, ctx_in, g_xattn, g_ffn, gamma, w_in, scale_in, scale1_in, out):
    x_t = x.rearrange("b c l -> (b c) l").rearrange("(t p) l -> t p l", p=P)
    c_t = ctx_in.rearrange("b c l -> (b c) l").rearrange("(t p) l -> t p l", p=P)
    out_t = out.rearrange("b c l -> (b c) l").rearrange("(t p) l -> t p l", p=P)
    w_k = w_in.rearrange("(k p) n -> p k n", p=P)

    def tile_of(dram, t, i):
        return dram[t, :, :] if i is None else dram[bass.ds(i * 2 + t, 1), :, :].rearrange("a p l -> (a p) l")

    es = ExitStack()
    with es:
        def sb(name, shape, dt=F32):
            return es.enter_context(nc.sbuf_tensor(name, shape, dt))

        def pb(name):
            return es.enter_context(nc.psum_tensor(name, [P, L], F32))

        def sem(name):
            return es.enter_context(nc.semaphore(name))

        stack = sb("stack", [P, 2, SLOTS, L], F32R)
        q_stack, k_stack = stack[:, 0, :, :], stack[:, 1, :, :]
        probs = sb("probs", [P, 2, HEADS_PER_TILE, CHUNKS, L])
        x_in = sb("x_in", [P, 2, L])
        c_in = sb("c_in", [P, 2, L])
        halves = sb("halves", [P, 2, 4, L], F32R)
        q_hi, q_lo, k_hi, k_lo = (halves[:, :, n, :] for n in (Q_HI, Q_LO, K_HI, K_LO))
        v_in = sb("v_in", [P, 2, L])
        v_t = sb("v_t", [P, 2, CHUNKS, P])
        o_sb = sb("o_sb", [P, 2, L])
        den_sb = sb("den_sb", [P, 2, L])
        inv_rows = sb("inv_rows", [HEADS_PER_TILE, 2, L])
        inv_sb = sb("inv_sb", [P, 2, L])
        x_res = sb("x_res", [P, 2, L])
        x1 = sb("x1", [P, 2, L])
        z = sb("z", [P, 2, L])
        magic = sb("magic", [P, 2, L])
        q8 = sb("q8", [P, 2, L], BF16)
        q8_t = sb("q8_t", [P, 2, CHUNKS, P], BF16)
        y_sb = sb("y_sb", [P, 2, L])
        den_col = sb("den_col", [P, 2, L * HEADS_PER_TILE // P])
        neg_max = sb("neg_max", [P, 2, UNITS])
        max_rows = sb("max_rows", [UNITS, 2, P])
        stats = sb("stats", [P, 4, nc.vector.BN_STATS_DIM])
        moments = sb("moments", [P, 4, 2])
        rstd = sb("rstd", [P, 4, 1])
        minus_half = sb("minus_half", [P, 1])
        eps = sb("eps", [P, 1])
        biggest = sb("biggest", [P, 2, 3])
        ffn_gain = sb("ffn_gain", [P, 2, 1])
        scalars = sb("scalars", [P, 5])
        gates = sb("gates", [P, 2])
        recips = sb("recips", [P, 2])
        att_gain = sb("att_gain", [P, 1])
        ffn_scale = sb("ffn_scale", [P, 2])
        w_f = sb("w_f", [P, CHUNKS, L])
        w_m = magic_w = sb("w_m", [P, L])
        w_n = sb("w_n", [P, L])
        w8 = sb("w8", [P, CHUNKS, L], BF16)
        ident = sb("ident", [P, P])
        ident16 = sb("ident16", [P, P], BF16)
        ones = sb("ones", [P, D])

        ps_st = [pb(f"ps_st{n}") for n in range(2)]
        ps_s = [pb(f"ps_s{n}") for n in range(2)]
        ps_o = pb("ps_o")
        ps_den = pb("ps_den")
        ps_small = pb("ps_small")
        ps_y = pb("ps_y")

        x_loaded = [sem(f"x_loaded{n}") for n in range(2)]
        c_loaded = [sem(f"c_loaded{n}") for n in range(2)]
        v_loaded = [sem(f"v_loaded{n}") for n in range(2)]
        res_loaded = [sem(f"res_loaded{n}") for n in range(2)]
        stacked = [sem(f"stacked{n}") for n in range(BODY)]
        max_stacked = [sem(f"max_stacked{n}") for n in range(BODY)]
        den_spread = sem("den_spread")
        inv_gathered = sem("inv_gathered")
        inv_broadcast = sem("inv_broadcast")
        y_sb_free = [sem(f"y_sb_free{n}") for n in range(2)]
        small_loaded = sem("small_loaded")
        w_loaded = sem("w_loaded")
        st_ready = sem("st_ready")
        s_ready = sem("s_ready")
        max_t_ready = sem("max_t_ready")
        v_t_ready = sem("v_t_ready")
        pv_done = sem("pv_done")
        q8_t_ready = sem("q8_t_ready")
        y_ready = sem("y_ready")
        probs_ready = sem("probs_ready")
        max_rows_ready = sem("max_rows_ready")
        v_t_saved = sem("v_t_saved")
        q8_t_saved = sem("q8_t_saved")
        o_saved = sem("o_saved")
        den_saved = sem("den_saved")
        k_hi_ready = sem("k_hi_ready")
        q_hi_ready = sem("q_hi_ready")
        gates_ready = sem("gates_ready")
        maxed = sem("maxed")
        stats_ready = sem("stats_ready")
        moments_ready = sem("moments_ready")
        q_normed = sem("q_normed")
        inv_ready = sem("inv_ready")
        x1_ready = sem("x1_ready")
        stats2_ready = sem("stats2_ready")
        moments2_ready = sem("moments2_ready")
        z_ready = sem("z_ready")
        exponent_ready = sem("exponent_ready")
        biggest_ready = sem("biggest_ready")
        gain_ready = sem("gain_ready")
        y_added = sem("y_added")
        weights_ready = sem("weights_ready")
        w_chain = sem("w_chain")
        ident16_ready = sem("ident16_ready")
        constants_ready = sem("constants_ready")
        ident_zeroed = sem("ident_zeroed")
        rstd_ready = sem("rstd_ready")
        rstd2_ready = sem("rstd2_ready")
        rstd2_scaled = sem("rstd2_scaled")
        k_lo_ready = sem("k_lo_ready")
        q_lo_ready = sem("q_lo_ready")
        o_normed = sem("o_normed")
        magic_ready = sem("magic_ready")
        rounded_up = sem("rounded_up")
        q8_ready = sem("q8_ready")
        var_ready = sem("var_ready")
        var2_ready = sem("var2_ready")

        block = es.enter_context(nc.Block())

        @block.sync
        def _(sp):
            for n, src in enumerate((g_xattn, g_ffn, gamma, scale_in, scale1_in)):
                sp.dma_start(scalars[:, n:n + 1], src.unsqueeze(0).to_broadcast([P, 1])).then_inc(small_loaded, DMA)

            def step(s, i):
                even, b4 = s % 2 == 0, s % BODY
                t = (s + 6) // 2
                if even and (i is None or t < TILES) and runs(t, i, TILES, 2):
                    upto(sp, q_normed, t - 1, i, 2)
                    sp.dma_start(x_in[:, t % 2, :], tile_of(x_t, t, i)).then_inc(x_loaded[t % 2], DMA)
                    upto(sp, k_hi_ready, t - 1, i, 2)
                    upto(sp, k_lo_ready, t - 1, i, 2)
                    sp.dma_start(c_in[:, t % 2, :], tile_of(c_t, t, i)).then_inc(c_loaded[t % 2], DMA)
                if s == FIRST_STEP + 2:
                    sp.dma_start(w_f[:, :, :], w_k).then_inc(w_loaded, DMA)
                if runs(s + 1, i, STEPS, BODY):
                    n = s + 1
                    upto(sp, max_rows_ready, n + 1, i, BODY)
                    slot = PAIR * (n % BODY)
                    sp.dma_start(q_stack[ONES_ROW:ONES_ROW + 1, slot:slot + PAIR, :].bitcast(F32),
                                 max_rows[:, n % 2, :]).then_inc(max_stacked[n % BODY], DMA)
                n = s + 3
                if runs(n, i, STEPS, BODY):
                    t = n // 2
                    upto(sp, st_ready, UNITS * (n - 3), i, UNITS * BODY)
                    for ready in (q_hi_ready, q_lo_ready, k_hi_ready, k_lo_ready):
                        upto(sp, ready, t + 1, i, 2)
                    for j in range(PAIR):
                        row = D * (PAIR * (n % 2) + j)
                        slot = PAIR * (n % BODY) + j
                        for place, (q_part, k_part) in enumerate(STACKED):
                            both = slice(q_part, k_part + 1, k_part - q_part)
                            sp.dma_start(stack[D * place:D * place + D, :, slot, :].bitcast(F32),
                                         halves[row:row + D, t % 2, both, :].bitcast(F32)
                                         ).then_inc(stacked[n % BODY], DMA)
                t = (s + 1) // 2
                if not even and runs(t, i, TILES, 2):
                    upto(sp, v_t_ready, t - 1, i, 2)
                    sp.dma_start(v_in[:, t % 2, :], tile_of(c_t, t, i)).then_inc(v_loaded[t % 2], DMA)
                t = (s - 4) // 2
                if even and runs(t, i, TILES, 2):
                    upto(sp, x1_ready, t - 1, i, 2)
                    sp.dma_start(x_res[:, t % 2, :], tile_of(x_t, t, i)).then_inc(res_loaded[t % 2], DMA)
                    upto(sp, den_saved, t + 1, i, 2)
                    sp.dma_start(den_col[:, t % 2, :], den_sb[0:P:D, t % 2, :]).then_inc(den_spread, DMA)
                t = (s - 5) // 2
                if not even and runs(t, i, TILES, 2):
                    upto(sp, inv_ready, t + 1, i, 2)
                    sp.dma_start(inv_rows[:, t % 2, :], den_col[:, t % 2, :]).then_inc(inv_gathered, DMA)
                    upto(sp, inv_gathered, DMA * (t + 1), i, 2 * DMA)
                    upto(sp, o_normed, t - 1, i, 2)
                    sp.dma_start(inv_sb[:, t % 2, :], inv_rows[:, t % 2, :].unsqueeze(1).to_broadcast(
                        [HEADS_PER_TILE, D, L])).then_inc(inv_broadcast, DMA)
                t = (s - 10) // 2
                if even and runs(t, i, TILES, 2):
                    upto(sp, y_added, t + 1, i, 2)
                    sp.dma_start(tile_of(out_t, t, i), y_sb[:, t % 2, :]).then_inc(y_sb_free[t % 2], DMA)

            steps(sp, step)
            for n in range(2):
                sp.wait_ge(y_sb_free[n], DMA * (TILES // 2 + 1))

        @block.gpsimd
        def _(pool):
            nc.gpsimd.memset(minus_half[:], -0.5).then_inc(constants_ready, 1)
            nc.gpsimd.memset(eps[:], LN_EPS).then_inc(constants_ready, 1)
            nc.gpsimd.memset(ones[:], 1.0).then_inc(constants_ready, 1)
            nc.gpsimd.memset(ident[:], 0.0).then_inc(ident_zeroed, 1)
            pool.wait_ge(ident_zeroed, 1)
            nc.gpsimd.affine_select(out=ident[:], in_=ident[:], compare_op=ALU.not_equal, fill=1.0, base=0,
                                    pattern=[[-1, P]], channel_multiplier=1).then_inc(constants_ready, 1)
            pool.wait_ge(constants_ready, 4)
            nc.gpsimd.memset(k_stack[ONES_ROW:ONES_ROW + 1, :, :].bitcast(F32), 1.0).then_inc(constants_ready, 1)
            pool.wait_ge(constants_ready, 5)
            for n in range(2):
                nc.gpsimd.memset(y_sb[:, n, 0:1], 0.0).then_inc(y_sb_free[n], DMA)
            pool.wait_ge(small_loaded, 5 * DMA)

            def inverse_deviation(eng_wait, count, i, n, var_sem, done):
                upto(pool, eng_wait, count, i, 2)
                nc.gpsimd.tensor_tensor(rstd[:, n, :], moments[:, n, 1:2], eps[:], ALU.add).then_inc(var_sem, 1)
                upto(pool, var_sem, count, i, 2)
                nc.gpsimd.tensor_tensor(rstd[:, n, :], rstd[:, n, :], minus_half[:], ALU.pow).then_inc(done, 1)

            def step(s, i):
                even = s % 2 == 0
                t = (s + 5) // 2
                if not even and runs(t, i, TILES, 2):
                    inverse_deviation(moments_ready, t + 1, i, t % 2, var_ready, rstd_ready)
                t = (s + 4) // 2
                if even and runs(t, i, TILES, 2):
                    upto(pool, k_hi_ready, t + 1, i, 2)
                    for n in (2 * t - 4, 2 * t - 3):
                        upto(pool, stacked[n % BODY], DMA * STACK_DMAS * (n // BODY + 1), i, DMA * STACK_DMAS)
                    nc.gpsimd.tensor_tensor(k_lo[:, t % 2, :], c_in[:, t % 2, :], k_hi[:, t % 2, :].bitcast(F32),
                                            ALU.subtract).then_inc(k_lo_ready, 1)
                    upto(pool, q_hi_ready, t + 1, i, 2)
                    nc.gpsimd.tensor_tensor(q_lo[:, t % 2, :], x_in[:, t % 2, :], q_hi[:, t % 2, :].bitcast(F32),
                                            ALU.subtract).then_inc(q_lo_ready, 1)
                t = (s - 6) // 2
                if even and runs(t, i, TILES, 2):
                    inverse_deviation(moments2_ready, t + 1, i, 2 + t % 2, var2_ready, rstd2_ready)
                    upto(pool, rstd2_ready, t + 1, i, 2)
                    nc.gpsimd.tensor_tensor(rstd[:, 2 + t % 2, :], rstd[:, 2 + t % 2, :], scalars[:, 3:4],
                                            ALU.mult).then_inc(rstd2_scaled, 1)
                t = (s - 7) // 2
                if not even and runs(t, i, TILES, 2):
                    m, zz = magic[:, t % 2, :], z[:, t % 2, :]
                    upto(pool, magic_ready, t + 1, i, 2)
                    nc.gpsimd.tensor_tensor(zz, zz, m, ALU.add).then_inc(rounded_up, 1)
                    upto(pool, rounded_up, t + 1, i, 2)
                    upto(pool, q8_t_ready, t - 1, i, 2)
                    upto(pool, biggest_ready, t - 1, i, 2)
                    nc.gpsimd.tensor_tensor(q8[:, t % 2, :], zz, m, ALU.subtract).then_inc(q8_ready, 1)
                t = (s - 5) // 2
                if not even and runs(t, i, TILES, 2):
                    upto(pool, o_saved, t + 1, i, 2)
                    upto(pool, inv_broadcast, DMA * (t + 1), i, 2 * DMA)
                    nc.gpsimd.tensor_tensor(o_sb[:, t % 2, :], o_sb[:, t % 2, :], inv_sb[:, t % 2, :],
                                            ALU.mult).then_inc(o_normed, 1)

            steps(pool, step)

        @block.scalar
        def _(act):
            act.wait_ge(small_loaded, 5 * DMA)
            nc.scalar.activation(gates[:], scalars[:, 0:2], ACT.Tanh).then_inc(gates_ready, 1)

            def step(s, i):
                even = s % 2 == 0

                def free_attention_banks():
                    t = (s - 4) // 2
                    if even and runs(t, i, TILES, 2):
                        upto(act, pv_done, t + 1, i, 2)
                        upto(act, x1_ready, t - 1, i, 2)
                        nc.scalar.copy(o_sb[:, t % 2, :], ps_o[:]).then_inc(o_saved, 1)
                        upto(act, den_spread, DMA * (t - 1), i, 2 * DMA)
                        nc.scalar.copy(den_sb[:, t % 2, :], ps_den[:]).then_inc(den_saved, 1)

                def save_max_rows():
                    n = s + 1
                    if runs(n, i, STEPS, BODY):
                        upto(act, max_t_ready, n + 1, i, BODY)
                        if i is not None or n >= 2:
                            upto(act, max_stacked[(n - 2) % BODY], DMA * ((n - 2) // BODY + 1), i, DMA)
                        nc.scalar.copy(max_rows[:, n % 2, :], ps_small[0:UNITS, 0:P]).then_inc(max_rows_ready, 1)

                def split_k():
                    t = (s + 4) // 2
                    if even and runs(t, i, TILES, 2):
                        upto(act, c_loaded[t % 2], DMA * (t // 2 + 1), i, DMA)
                        for n in (2 * t - 4, 2 * t - 3):
                            upto(act, stacked[n % BODY], DMA * STACK_DMAS * (n // BODY + 1), i, DMA * STACK_DMAS)
                        nc.scalar.copy(k_hi[:, t % 2, :], c_in[:, t % 2, :]).then_inc(k_hi_ready, 1)

                def split_q():
                    t = (s + 4) // 2
                    if even and runs(t, i, TILES, 2):
                        upto(act, q_normed, t + 1, i, 2)
                        nc.scalar.copy(q_hi[:, t % 2, :], x_in[:, t % 2, :]).then_inc(q_hi_ready, 1)

                def save_v():
                    t = s // 2
                    if even and runs(t, i, TILES, 2):
                        upto(act, v_t_ready, t + 1, i, 2)
                        upto(act, pv_done, t - 1, i, 2)
                        nc.scalar.copy(v_t[:, t % 2, :, :], ps_small[:].rearrange("p (c r) -> p c r", c=CHUNKS)
                                       ).then_inc(v_t_saved, 1)

                def save_q8():
                    t = (s - 9) // 2
                    if not even and runs(t, i, TILES, 2):
                        upto(act, q8_t_ready, t + 1, i, 2)
                        nc.scalar.copy(q8_t[:, t % 2, :, :], ps_small.ap().bitcast(BF16)[:, 0:L].rearrange(
                            "p (c r) -> p c r", c=CHUNKS)).then_inc(q8_t_saved, 1)

                def exponentials(u):
                    if runs(s, i, STEPS, BODY):
                        upto(act, st_ready, UNITS * s + u + 1, i, UNITS * BODY)
                        t = s // 2
                        if u == 0:
                            upto(act, pv_done, t - 1, i, 2)
                        nc.scalar.activation(probs[:, t % 2, PAIR * (s % 2) + u // CHUNKS, u % CHUNKS, :],
                                             ps_st[u % 2][:], ACT.Exp, scale=SM_SCALE).then_inc(probs_ready, 1)

                free_attention_banks()
                exponentials(0)
                save_max_rows()
                exponentials(1)
                split_k()
                exponentials(2)
                exponentials(3)
                split_q()
                exponentials(4)
                save_v()
                exponentials(5)
                save_q8()
                exponentials(6)
                exponentials(7)

            steps(act, step)

        @block.vector
        def _(dve):
            dve.wait_ge(constants_ready, 5)
            nc.vector.tensor_copy(ident16[:], ident[:]).then_inc(ident16_ready, 1)
            chain = [0]

            def link(ins):
                chain[0] += 1
                ins.then_inc(w_chain, 1)
                dve.wait_ge(w_chain, chain[0])

            def gains():
                dve.wait_ge(small_loaded, 5 * DMA)
                link(nc.vector.reciprocal(recips[:], scalars[:, 3:5]))
                dve.wait_ge(gates_ready, 1)
                nc.vector.tensor_scalar(att_gain[:], gates[:, 0:1], scalars[:, 2:3], None, ALU.mult)
                link(nc.vector.tensor_scalar(ffn_scale[:, 0:1], gates[:, 1:2], recips[:, 0:1], recips[:, 1:2],
                                             ALU.mult, ALU.mult))

            def round_weights(c):
                w = w_f[:, c, :]
                if c == 0:
                    dve.wait_ge(w_loaded, DMA)
                link(nc.vector.tensor_scalar(w, w, scalars[:, 4:5], None, ALU.mult))
                link(nc.vector.tensor_scalar(w_m[:].bitcast(U32), w.bitcast(U32), EXPONENT_BITS, None,
                                             ALU.bitwise_and))
                link(nc.vector.tensor_scalar(w_m[:], w_m[:], ROUND_AT, ROUND_LEAST, ALU.mult, ALU.max))
                link(nc.vector.tensor_tensor(w, w, w_m[:], ALU.add))
                link(nc.vector.tensor_tensor(w, w, w_m[:], ALU.subtract))
                link(nc.vector.tensor_tensor(w_n[:], w, w, ALU.mult))
                link(nc.vector.tensor_scalar(w_n[:], w_n[:], FP8_MAX * FP8_MAX, HUGE, ALU.is_gt, ALU.mult))
                link(nc.vector.tensor_scalar(w_n[:], w_n[:], HUGE, None, ALU.mult))
                link(nc.vector.tensor_tensor(w_n[:], w_n[:], w_n[:], ALU.subtract))
                nc.vector.tensor_tensor(w8[:, c, :], w, w_n[:], ALU.add).then_inc(weights_ready, 1)
                dve.wait_ge(weights_ready, c + 1)

            def step(s, i):
                even = s % 2 == 0

                def maximum(u):
                    n = s + 2
                    if runs(n, i, STEPS, BODY):
                        upto(dve, s_ready, UNITS * n + u + 1, i, UNITS * BODY)
                        if u == 0:
                            upto(dve, max_t_ready, n - 1, i, BODY)
                        nc.vector.tensor_reduce(neg_max[:, n % 2, u:u + 1], ps_s[u % 2][:], AX, ALU.max,
                                                negate=True).then_inc(maxed, 1)

                def measure_x():
                    t = (s + 5) // 2
                    if not even and runs(t, i, TILES, 2):
                        upto(dve, x_loaded[t % 2], DMA * (t // 2 + 1), i, DMA)
                        nc.vector.bn_stats(stats[:, t % 2, :], x_in[:, t % 2, :]).then_inc(stats_ready, 1)
                        upto(dve, stats_ready, t + 1, i, 2)

                def moments_of_x():
                    t = (s + 5) // 2
                    if not even and runs(t, i, TILES, 2):
                        nc.vector.bn_aggr(moments[:, t % 2, :], stats[:, t % 2, :]).then_inc(moments_ready, 1)

                def normalise_x():
                    t = (s + 4) // 2
                    if even and runs(t, i, TILES, 2):
                        upto(dve, rstd_ready, t + 1, i, 2)
                        nc.vector.tensor_scalar(x_in[:, t % 2, :], x_in[:, t % 2, :], moments[:, t % 2, 0:1],
                                                rstd[:, t % 2, :], ALU.subtract, ALU.mult).then_inc(q_normed, 1)

                def invert_sums():
                    t = (s - 5) // 2
                    if not even and runs(t, i, TILES, 2):
                        upto(dve, den_spread, DMA * (t + 1), i, 2 * DMA)
                        nc.vector.reciprocal(den_col[:, t % 2, :], den_col[:, t % 2, :]).then_inc(inv_ready, 1)

                def add_attention():
                    t = (s - 6) // 2
                    if even and runs(t, i, TILES, 2):
                        upto(dve, o_normed, t + 1, i, 2)
                        upto(dve, y_added, t - 1, i, 2)
                        upto(dve, res_loaded[t % 2], DMA * (t // 2 + 1), i, DMA)
                        nc.vector.scalar_tensor_tensor(out=x1[:, t % 2, :], in0=o_sb[:, t % 2, :], scalar=att_gain[:],
                                                       in1=x_res[:, t % 2, :], op0=ALU.mult,
                                                       op1=ALU.add).then_inc(x1_ready, 1)

                def measure_x1():
                    t = (s - 6) // 2
                    if even and runs(t, i, TILES, 2):
                        upto(dve, x1_ready, t + 1, i, 2)
                        nc.vector.bn_stats(stats[:, 2 + t % 2, :], x1[:, t % 2, :]).then_inc(stats2_ready, 1)
                        upto(dve, stats2_ready, t + 1, i, 2)

                def moments_of_x1():
                    t = (s - 6) // 2
                    if even and runs(t, i, TILES, 2):
                        nc.vector.bn_aggr(moments[:, 2 + t % 2, :], stats[:, 2 + t % 2, :]
                                          ).then_inc(moments2_ready, 1)

                def normalise_x1():
                    t = (s - 7) // 2
                    if not even and runs(t, i, TILES, 2):
                        upto(dve, rstd2_scaled, t + 1, i, 2)
                        nc.vector.tensor_scalar(z[:, t % 2, :], x1[:, t % 2, :], moments[:, 2 + t % 2, 0:1],
                                                rstd[:, 2 + t % 2, :], ALU.subtract, ALU.mult).then_inc(z_ready, 1)

                def powers_of_two():
                    t = (s - 7) // 2
                    if not even and runs(t, i, TILES, 2):
                        upto(dve, z_ready, t + 1, i, 2)
                        nc.vector.tensor_scalar(magic[:, t % 2, :].bitcast(U32), z[:, t % 2, :].bitcast(U32),
                                                EXPONENT_BITS, None, ALU.bitwise_and).then_inc(exponent_ready, 1)

                def magic_numbers():
                    t = (s - 7) // 2
                    if not even and runs(t, i, TILES, 2):
                        upto(dve, exponent_ready, t + 1, i, 2)
                        nc.vector.tensor_scalar(magic[:, t % 2, :], magic[:, t % 2, :], ROUND_AT, ROUND_LEAST,
                                                ALU.mult, ALU.max).then_inc(magic_ready, 1)

                def gain_of_rows():
                    t = (s - 9) // 2
                    if not even and runs(t, i, TILES, 2):
                        n = t % 2
                        upto(dve, q8_ready, t + 1, i, 2)
                        nc.vector.tensor_reduce(biggest[:, n, 0:1], q8[:, n, :], AX, ALU.max,
                                                apply_absolute_value=True).then_inc(biggest_ready, 1)
                        upto(dve, biggest_ready, t + 1, i, 2)
                        nc.vector.tensor_scalar(biggest[:, n, 1:2], biggest[:, n, 0:1], FP8_MAX, HUGE,
                                                ALU.is_gt, ALU.mult).then_inc(gain_ready, 1)
                        upto(dve, gain_ready, 3 * t + 1, i, 6)
                        nc.vector.tensor_scalar(biggest[:, n, 2:3], biggest[:, n, 1:2], HUGE, None,
                                                ALU.mult).then_inc(gain_ready, 1)
                        upto(dve, gain_ready, 3 * t + 2, i, 6)
                        nc.vector.scalar_tensor_tensor(out=ffn_gain[:, n, :], in0=biggest[:, n, 2:3],
                                                       scalar=biggest[:, n, 2:3], in1=ffn_scale[:, 0:1],
                                                       op0=ALU.subtract, op1=ALU.add).then_inc(gain_ready, 1)

                def add_product():
                    t = (s - 10) // 2
                    if even and runs(t, i, TILES, 2):
                        upto(dve, y_ready, t + 1, i, 2)
                        upto(dve, gain_ready, 3 * t + 3, i, 6)
                        upto(dve, y_sb_free[t % 2], DMA * (t // 2 + 1), i, DMA)
                        nc.vector.scalar_tensor_tensor(out=y_sb[:, t % 2, :], in0=ps_y[:], scalar=ffn_gain[:, t % 2, :],
                                                       in1=x1[:, t % 2, :], op0=ALU.mult,
                                                       op1=ALU.add).then_inc(y_added, 1)

                normalise_x()
                maximum(0)
                add_product()
                invert_sums()
                maximum(1)
                normalise_x1()
                maximum(2)
                add_attention()
                powers_of_two()
                maximum(3)
                measure_x1()
                magic_numbers()
                maximum(4)
                moments_of_x1()
                measure_x()
                maximum(5)
                moments_of_x()
                gain_of_rows()
                maximum(6)
                maximum(7)
                if s == 1:
                    gains()
                if s in (1, 2, 3, 5):
                    round_weights((1, 2, 3, 5).index(s))

            steps(dve, step)

        @block.tensor
        def _(pe):
            pe.wait_ge(constants_ready, 5)
            pe.wait_ge(ident16_ready, 1)

            def step(s, i):
                even = s % 2 == 0

                def scores_t(u):
                    if runs(s, i, STEPS, BODY):
                        slot, c = PAIR * (s % BODY) + u // CHUNKS, u % CHUNKS
                        if u == 0:
                            upto(pe, max_stacked[s % BODY], DMA * (s // BODY + 1), i, DMA)
                        upto(pe, probs_ready, UNITS * s + u - 1, i, UNITS * BODY)
                        nc.tensor.matmul(ps_st[u % 2][:], k_stack[0:ONES_ROW + 1, slot, c * P:(c + 1) * P],
                                         q_stack[0:ONES_ROW + 1, slot, :], start=True, stop=True
                                         ).then_inc(st_ready, 1)

                def scores(u):
                    n = s + 2
                    if runs(n, i, STEPS, BODY):
                        slot, c = PAIR * (n % BODY) + u // CHUNKS, u % CHUNKS
                        if u == 0:
                            upto(pe, stacked[n % BODY], DMA * STACK_DMAS * (n // BODY + 1), i, DMA * STACK_DMAS)
                        upto(pe, maxed, UNITS * n + u - 1, i, UNITS * BODY)
                        nc.tensor.matmul(ps_s[u % 2][:], q_stack[0:ONES_ROW, slot, c * P:(c + 1) * P],
                                         k_stack[0:ONES_ROW, slot, :], start=True, stop=True).then_inc(s_ready, 1)

                def attend(g):
                    t, c = (s - 2) // 2, 2 * (s % 2) + g // 2
                    if runs(t, i, TILES, 2):
                        if g % 2 == 0:
                            upto(pe, probs_ready, 2 * UNITS * (t + 1) - CHUNKS + c + 1, i, 4 * UNITS)
                        if g == 0 and even:
                            upto(pe, v_t_saved, t + 1, i, 2)
                            upto(pe, o_saved, t, i, 2)
                            upto(pe, den_saved, t, i, 2)
                        for h in range(HEADS_PER_TILE):
                            rows = slice(D * h, D * h + D)
                            moving = probs[:, t % 2, h, c, :]
                            if g % 2 == 0:
                                last = nc.tensor.matmul(ps_o[rows, :], v_t[:, t % 2, c, rows], moving,
                                                        start=c == 0, stop=c == CHUNKS - 1)
                            else:
                                last = nc.tensor.matmul(ps_den[rows, :], ones[:], moving,
                                                        start=c == 0, stop=c == CHUNKS - 1)
                        if c == CHUNKS - 1 and g % 2 == 1:
                            last.then_inc(pv_done, 1)

                def transpose_max():
                    n = s + 1
                    if runs(n, i, STEPS, BODY):
                        upto(pe, maxed, UNITS * (n + 1), i, UNITS * BODY)
                        upto(pe, max_rows_ready, n, i, BODY)
                        if even:
                            upto(pe, q8_t_saved, (s - 10) // 2 + 1, i, 2)
                        else:
                            upto(pe, v_t_saved, (s - 1) // 2 + 1, i, 2)
                        nc.tensor.transpose(ps_small[0:UNITS, 0:P], neg_max[:, n % 2, :], ident[:]
                                            ).then_inc(max_t_ready, 1)

                def transpose_v():
                    t = s // 2
                    if even and runs(t, i, TILES, 2):
                        upto(pe, v_loaded[t % 2], DMA * (t // 2 + 1), i, DMA)
                        upto(pe, max_rows_ready, s + 2, i, BODY)
                        for c in range(CHUNKS):
                            last = nc.tensor.transpose(ps_small[:, c * P:(c + 1) * P],
                                                       v_in[:, t % 2, c * P:(c + 1) * P], ident[:])
                        last.then_inc(v_t_ready, 1)

                def transpose_q8():
                    t = (s - 9) // 2
                    if not even and runs(t, i, TILES, 2):
                        upto(pe, q8_ready, t + 1, i, 2)
                        upto(pe, max_rows_ready, min(s + 2, STEPS) if i is None else s + 2, i, BODY)
                        upto(pe, v_t_saved, min((s - 1) // 2 + 1, TILES) if i is None else (s - 1) // 2 + 1, i, 2)
                        upto(pe, q8_t_saved, t, i, 2)
                        for c in range(CHUNKS):
                            last = nc.tensor.transpose(ps_small.ap().bitcast(BF16)[:, c * P:(c + 1) * P],
                                                       q8[:, t % 2, c * P:(c + 1) * P], ident16[:])
                        last.then_inc(q8_t_ready, 1)

                def product():
                    t = (s - 9) // 2
                    if not even and runs(t, i, TILES, 2):
                        upto(pe, q8_t_saved, t + 1, i, 2)
                        upto(pe, y_added, t, i, 2)
                        if t == 0:
                            upto(pe, weights_ready, CHUNKS, None, 0)
                        for c in range(CHUNKS):
                            last = nc.tensor.matmul(ps_y[:], q8_t[:, t % 2, c, :], w8[:, c, :],
                                                    start=c == 0, stop=c == CHUNKS - 1)
                        last.then_inc(y_ready, 1)

                for u in range(UNITS):
                    scores_t(u)
                    scores(u)
                    if u == 0:
                        transpose_max()
                    if u % 2 == 1:
                        attend(u // 2)
                    if u == 2:
                        transpose_v()
                    if u == 3:
                        transpose_q8()
                    if u == 5:
                        product()

            steps(pe, step)


_INS = ["x", "ctx_2048", "g_xattn", "g_ffn", "L0_xattn_gamma", "L0_ffn_input2", "L0_ffn_scale", "L0_ffn_scale1"]


def kernel(**inputs):
    import numpy as _np
    import concourse.bacc as _bacc
    from concourse import mybir as _mybir
    from concourse.bass_utils import run_bass_kernel_spmd as _run

    nc = _bacc.Bacc("TRN2", target_bir_lowering=False, num_devices=1)
    arrays, args = {}, []
    for name in _INS:
        a = _np.ascontiguousarray(inputs[name])
        arrays[f"in_{name}"] = a
        args.append(nc.dram_tensor(f"in_{name}", a.shape, _mybir.dt.from_np(a.dtype), kind="ExternalInput").ap())
    args.append(nc.dram_tensor("out_x", (IMAGES, CHANNELS, L), F32, kind="ExternalOutput").ap())
    build(nc, *args)
    r = _run(nc, [arrays], core_ids=[0])
    return r.results[0]["out_x"]
```

```python
from contextlib import ExitStack

import concourse.bass as bass
from concourse import mybir

F32 = mybir.dt.float32
F32R = mybir.dt.float32r
BF16 = mybir.dt.bfloat16
F16 = mybir.dt.float16
U32 = mybir.dt.uint32
ALU = mybir.AluOpType
ACT = mybir.ActivationFunctionType
AX = mybir.AxisListType.X

P = 128
L = 512
D = 32
IMAGES, CHANNELS = 8, 256
TILES = IMAGES * CHANNELS // P
HEADS_PER_TILE = P // D
PAIR = 2
STEPS = TILES * HEADS_PER_TILE // PAIR
CHUNKS = L // P
UNITS = PAIR * CHUNKS
SLOTS = 2 * HEADS_PER_TILE
ONES_ROW = 3 * D
Q_HI, Q_LO, K_HI, K_LO = range(4)
STACKED = ((Q_HI, K_HI), (Q_LO, K_HI), (Q_HI, K_LO))
STACK_DMAS = PAIR * len(STACKED)
LN_EPS = 1e-5
SM_SCALE = float(D) ** -0.5
CONSTANTS = 6
DMA = 16

EXPONENT_BITS = 0x7F800000
ROUND_AT = 1.5 * 2.0 ** 20
ROUND_LEAST = ROUND_AT * 2.0 ** -6
FP16_GUARD = 144.0

FIRST_STEP, LOOP_FIRST, LOOPS, LAST_STEP = -6, 10, 4, STEPS + 10
BODY = 4


def upto(eng, sem, count, i, per_loop):
    if i is None:
        if count > 0:
            eng.wait_ge(sem, count)
    else:
        assert count > 0
        eng.wait_ge(sem, i * per_loop + count)


def runs(index, i, n, per_loop):
    if i is None:
        return 0 <= index < n
    assert index >= 0 and index + per_loop * (LOOPS - 1) < n
    return True


def steps(eng, step):
    for s in range(FIRST_STEP, LOOP_FIRST):
        step(s, None)
    with eng.Fori(0, LOOPS) as i:
        for s in range(LOOP_FIRST, LOOP_FIRST + BODY):
            step(s, i)
    for s in range(LOOP_FIRST + BODY * LOOPS, LAST_STEP):
        step(s, None)


def build(nc, x, ctx_in, g_xattn, g_ffn, gamma, w_in, scale_in, scale1_in, out):
    x_t = x.rearrange("b c l -> (b c) l").rearrange("(t p) l -> t p l", p=P)
    c_t = ctx_in.rearrange("b c l -> (b c) l").rearrange("(t p) l -> t p l", p=P)
    out_t = out.rearrange("b c l -> (b c) l").rearrange("(t p) l -> t p l", p=P)
    w_k = w_in.rearrange("(k p) n -> p k n", p=P)

    def tile_of(dram, t, i):
        return dram[t, :, :] if i is None else dram[bass.ds(i * 2 + t, 1), :, :].rearrange("a p l -> (a p) l")

    es = ExitStack()
    with es:
        def sb(name, shape, dt=F32):
            return es.enter_context(nc.sbuf_tensor(name, shape, dt))

        def pb(name):
            return es.enter_context(nc.psum_tensor(name, [P, L], F32))

        def sem(name):
            return es.enter_context(nc.semaphore(name))

        stack = sb("stack", [P, 2, SLOTS, L], F32R)
        q_stack, k_stack = stack[:, 0, :, :], stack[:, 1, :, :]
        probs = sb("probs", [P, 2, HEADS_PER_TILE, CHUNKS, L])
        pair_sums = sb("pair_sums", [P, 2, HEADS_PER_TILE, L])
        x_in = sb("x_in", [P, 2, L])
        c_in = sb("c_in", [P, 2, L])
        halves = sb("halves", [P, 2, 4, L], F32R)
        q_hi, q_lo, k_hi, k_lo = (halves[:, :, n, :] for n in (Q_HI, Q_LO, K_HI, K_LO))
        v_in = sb("v_in", [P, L])
        v_t = sb("v_t", [P, 2, CHUNKS, P])
        o_sb = sb("o_sb", [P, 2, L])
        den_sb = sb("den_sb", [P, L])
        inv_rows = sb("inv_rows", [HEADS_PER_TILE, 2, L])
        inv_sb = sb("inv_sb", [P, 2, L])
        x_res = sb("x_res", [P, 2, L])
        x1 = sb("x1", [P, 2, L])
        z = sb("z", [P, 2, L])
        magic = sb("magic", [P, 2, L])
        q8 = sb("q8", [P, 2, L], BF16)
        q8_t = sb("q8_t", [P, 2, CHUNKS, P], F16)
        y_sb = sb("y_sb", [P, 2, L])
        den_col = sb("den_col", [P, 2, L * HEADS_PER_TILE // P])
        neg_max = sb("neg_max", [P, 2, UNITS])
        max_rows = sb("max_rows", [UNITS, 2, P])
        stats = sb("stats", [P, 4, nc.vector.BN_STATS_DIM])
        moments = sb("moments", [P, 4, 2])
        rstd = sb("rstd", [P, 4, 1])
        shift = sb("shift", [P, 4, 1])
        zero = sb("zero", [P, 1])
        zero16 = sb("zero16", [P, 1], BF16)
        minus_half = sb("minus_half", [P, 1])
        eps = sb("eps", [P, 1])
        ffn_gain = sb("ffn_gain", [P, 2, 1])
        scalars = sb("scalars", [P, 5])
        gates = sb("gates", [P, 2])
        recips = sb("recips", [P, 2])
        att_gain = sb("att_gain", [P, 1])
        ffn_scale = sb("ffn_scale", [P, 2])
        w_f = sb("w_f", [P, CHUNKS, L])
        w_magic = sb("w_magic", [P, CHUNKS, L])
        w_nan = sb("w_nan", [P, CHUNKS, L], F16)
        w8 = sb("w8", [P, CHUNKS, L], BF16)
        ident = sb("ident", [P, P])
        ident16 = sb("ident16", [P, P], BF16)
        ones = sb("ones", [P, D])

        ps_st = [pb(f"ps_st{n}") for n in range(2)]
        ps_s = [pb(f"ps_s{n}") for n in range(2)]
        ps_o = pb("ps_o")
        ps_den = pb("ps_den")
        ps_small = pb("ps_small")
        ps_y = pb("ps_y")

        x_loaded = [sem(f"x_loaded{n}") for n in range(2)]
        c_loaded = [sem(f"c_loaded{n}") for n in range(2)]
        v_loaded = sem("v_loaded")
        res_loaded = [sem(f"res_loaded{n}") for n in range(2)]
        stacked = [sem(f"stacked{n}") for n in range(BODY)]
        max_stacked = [sem(f"max_stacked{n}") for n in range(BODY)]
        den_spread = sem("den_spread")
        inv_gathered = sem("inv_gathered")
        inv_broadcast = sem("inv_broadcast")
        y_sb_free = [sem(f"y_sb_free{n}") for n in range(2)]
        small_loaded = sem("small_loaded")
        w_loaded = sem("w_loaded")
        st_ready = sem("st_ready")
        s_ready = sem("s_ready")
        max_t_ready = sem("max_t_ready")
        v_t_ready = sem("v_t_ready")
        pv_done = sem("pv_done")
        q8_t_ready = sem("q8_t_ready")
        nan_ready = sem("nan_ready")
        y_ready = sem("y_ready")
        probs_ready = sem("probs_ready")
        max_rows_ready = sem("max_rows_ready")
        v_t_saved = sem("v_t_saved")
        q8_t_saved = sem("q8_t_saved")
        o_saved = sem("o_saved")
        den_saved = sem("den_saved")
        k_hi_ready = sem("k_hi_ready")
        q_hi_ready = sem("q_hi_ready")
        gates_ready = sem("gates_ready")
        w_guarded = sem("w_guarded")
        maxed = sem("maxed")
        pairs_summed = sem("pairs_summed")
        stats_ready = sem("stats_ready")
        moments_ready = sem("moments_ready")
        q_normed = sem("q_normed")
        inv_ready = sem("inv_ready")
        x1_ready = sem("x1_ready")
        stats2_ready = sem("stats2_ready")
        moments2_ready = sem("moments2_ready")
        z_ready = sem("z_ready")
        exponent_ready = sem("exponent_ready")
        sums_inverted = sem("sums_inverted")
        gain_ready = sem("gain_ready")
        y_added = sem("y_added")
        gates_chain = sem("gates_chain")
        w_scaled = sem("w_scaled")
        w_exponent_ready = sem("w_exponent_ready")
        w_magic_ready = sem("w_magic_ready")
        w_nan_ready = sem("w_nan_ready")
        ident16_ready = sem("ident16_ready")
        weights_ready = sem("weights_ready")
        w_rounded_up = sem("w_rounded_up")
        w_rounded = sem("w_rounded")
        ones_row_ready = sem("ones_row_ready")
        constants_ready = sem("constants_ready")
        ident_zeroed = sem("ident_zeroed")
        rstd_ready = sem("rstd_ready")
        rstd2_ready = sem("rstd2_ready")
        rstd2_scaled = sem("rstd2_scaled")
        shift_product = sem("shift_product")
        shift_ready = sem("shift_ready")
        shift2_product = sem("shift2_product")
        shift2_ready = sem("shift2_ready")
        k_lo_ready = sem("k_lo_ready")
        q_lo_ready = sem("q_lo_ready")
        o_normed = sem("o_normed")
        magic_ready = sem("magic_ready")
        rounded_up = sem("rounded_up")
        q8_ready = sem("q8_ready")
        var_ready = sem("var_ready")
        var2_ready = sem("var2_ready")

        block = es.enter_context(nc.Block())

        @block.sync
        def _(sp):
            def step(s, i):
                even = s % 2 == 0

                def stack_head(j):
                    n = s + 3
                    if runs(n, i, STEPS, BODY):
                        t = n // 2
                        if j == 0:
                            upto(sp, st_ready, UNITS * (n - 3), i, UNITS * BODY)
                            for ready in (q_hi_ready, q_lo_ready, k_hi_ready, k_lo_ready):
                                upto(sp, ready, t + 1, i, 2)
                        row = D * (PAIR * (n % 2) + j)
                        slot = PAIR * (n % BODY) + j
                        for place, (q_part, k_part) in enumerate(STACKED):
                            both = slice(q_part, k_part + 1, k_part - q_part)
                            sp.dma_start(stack[D * place:D * place + D, :, slot, :].bitcast(F32),
                                         halves[row:row + D, t % 2, both, :].bitcast(F32)
                                         ).then_inc(stacked[n % BODY], DMA)

                def stack_max():
                    n = s + 1
                    if runs(n, i, STEPS, BODY):
                        upto(sp, max_rows_ready, n + 1, i, BODY)
                        slot = PAIR * (n % BODY)
                        sp.dma_start(q_stack[ONES_ROW:ONES_ROW + 1, slot:slot + PAIR, :].bitcast(F32),
                                     max_rows[:, n % 2, :]).then_inc(max_stacked[n % BODY], DMA)

                def spread_sums():
                    t = (s - 4) // 2
                    if even and runs(t, i, TILES, 2):
                        upto(sp, den_saved, t + 1, i, 2)
                        sp.dma_start(den_col[:, t % 2, :], den_sb[0:P:D, :]).then_inc(den_spread, DMA)

                def gather_sums():
                    t = (s - 5) // 2
                    if not even and runs(t, i, TILES, 2):
                        upto(sp, inv_ready, t + 1, i, 2)
                        sp.dma_start(inv_rows[:, t % 2, :], den_col[:, t % 2, :]).then_inc(inv_gathered, DMA)

                def broadcast_sums():
                    t = (s - 5) // 2
                    if not even and runs(t, i, TILES, 2):
                        upto(sp, inv_gathered, DMA * (t + 1), i, 2 * DMA)
                        upto(sp, o_normed, t - 1, i, 2)
                        sp.dma_start(inv_sb[:, t % 2, :], inv_rows[:, t % 2, :].unsqueeze(1).to_broadcast(
                            [HEADS_PER_TILE, D, L])).then_inc(inv_broadcast, DMA)

                def load():
                    t = (s + 6) // 2
                    if even and (i is None or t < TILES) and runs(t, i, TILES, 2):
                        upto(sp, q_lo_ready, t - 1, i, 2)
                        sp.dma_start(x_in[:, t % 2, :], tile_of(x_t, t, i)).then_inc(x_loaded[t % 2], DMA)
                        upto(sp, k_hi_ready, t - 1, i, 2)
                        upto(sp, k_lo_ready, t - 1, i, 2)
                        sp.dma_start(c_in[:, t % 2, :], tile_of(c_t, t, i)).then_inc(c_loaded[t % 2], DMA)

                def load_v():
                    t = (s + 1) // 2
                    if not even and runs(t, i, TILES, 2):
                        upto(sp, v_t_ready, t, i, 2)
                        sp.dma_start(v_in[:], tile_of(c_t, t, i)).then_inc(v_loaded, DMA)

                def load_residual():
                    t = (s - 4) // 2
                    if even and runs(t, i, TILES, 2):
                        upto(sp, x1_ready, t - 1, i, 2)
                        sp.dma_start(x_res[:, t % 2, :], tile_of(x_t, t, i)).then_inc(res_loaded[t % 2], DMA)

                def store():
                    t = (s - 10) // 2
                    if even and runs(t, i, TILES, 2):
                        upto(sp, y_added, t + 1, i, 2)
                        sp.dma_start(tile_of(out_t, t, i), y_sb[:, t % 2, :]).then_inc(y_sb_free[t % 2], DMA)

                stack_head(0)
                stack_max()
                spread_sums()
                gather_sums()
                stack_head(1)
                broadcast_sums()
                load()
                load_v()
                load_residual()
                store()
                if s == FIRST_STEP + 4:
                    for n, src in enumerate((g_xattn, g_ffn, gamma, scale_in, scale1_in)):
                        sp.dma_start(scalars[:, n:n + 1], src.unsqueeze(0).to_broadcast([P, 1])
                                     ).then_inc(small_loaded, DMA)
                    sp.dma_start(w_f[:, :, :], w_k).then_inc(w_loaded, DMA)

            steps(sp, step)
            for n in range(2):
                sp.wait_ge(y_sb_free[n], DMA * (TILES // 2 + 1))

        @block.gpsimd
        def _(pool):
            nc.gpsimd.memset(minus_half[:], -0.5).then_inc(constants_ready, 1)
            nc.gpsimd.memset(zero[:], 0.0).then_inc(constants_ready, 1)
            nc.gpsimd.memset(eps[:], LN_EPS).then_inc(constants_ready, 1)
            pool.wait_ge(constants_ready, 3)

            def constants():
                nc.gpsimd.memset(ones[:], 1.0).then_inc(constants_ready, 1)
                nc.gpsimd.memset(zero16[:], 0.0).then_inc(constants_ready, 1)
                nc.gpsimd.memset(ident[:], 0.0).then_inc(ident_zeroed, 1)
                pool.wait_ge(ident_zeroed, 1)
                nc.gpsimd.affine_select(out=ident[:], in_=ident[:], compare_op=ALU.not_equal, fill=1.0, base=0,
                                        pattern=[[-1, P]], channel_multiplier=1).then_inc(constants_ready, 1)
                for n in range(2):
                    nc.gpsimd.memset(y_sb[:, n, 0:1], 0.0).then_inc(y_sb_free[n], DMA)

            def round_weights(c):
                w, m = w_f[:, c, :], w_magic[:, c, :]
                pool.wait_ge(w_magic_ready, 1)
                nc.gpsimd.tensor_tensor(w, w, m, ALU.add).then_inc(w_rounded_up, 1)
                pool.wait_ge(w_rounded_up, c + 1)
                nc.gpsimd.tensor_tensor(w, w, m, ALU.subtract).then_inc(w_rounded, 1)

            def finish_weights(c):
                pool.wait_ge(w_nan_ready, c + 1)
                nc.gpsimd.tensor_tensor(w8[:, c, :], w_f[:, c, :], w_nan[:, c, :], ALU.add
                                        ).then_inc(weights_ready, 1)

            def inverse_deviation(measured, count, i, n, var_sem, done):
                upto(pool, measured, count, i, 2)
                nc.gpsimd.tensor_tensor(rstd[:, n, :], moments[:, n, 1:2], eps[:], ALU.add).then_inc(var_sem, 1)
                upto(pool, var_sem, count, i, 2)
                nc.gpsimd.tensor_tensor(rstd[:, n, :], rstd[:, n, :], minus_half[:], ALU.pow).then_inc(done, 1)

            def shift_of(scaled, count, i, n, product_sem, done):
                upto(pool, scaled, count, i, 2)
                nc.gpsimd.tensor_tensor(shift[:, n, :], moments[:, n, 0:1], rstd[:, n, :], ALU.mult
                                        ).then_inc(product_sem, 1)
                upto(pool, product_sem, count, i, 2)
                nc.gpsimd.tensor_tensor(shift[:, n, :], zero[:], shift[:, n, :], ALU.subtract).then_inc(done, 1)

            def step(s, i):
                even = s % 2 == 0
                if s == FIRST_STEP + 2:
                    constants()
                t = (s - 6) // 2
                if even and runs(t, i, TILES, 2):
                    upto(pool, o_normed, t + 1, i, 2)
                    upto(pool, y_added, t - 1, i, 2)
                    upto(pool, res_loaded[t % 2], DMA * (t // 2 + 1), i, DMA)
                    nc.gpsimd.tensor_tensor(x1[:, t % 2, :], o_sb[:, t % 2, :], x_res[:, t % 2, :],
                                            ALU.add).then_inc(x1_ready, 1)
                t = (s + 4) // 2
                if even and runs(t, i, TILES, 2):
                    upto(pool, k_hi_ready, t + 1, i, 2)
                    for n in (2 * t - 4, 2 * t - 3):
                        upto(pool, stacked[n % BODY], DMA * STACK_DMAS * (n // BODY + 1), i, DMA * STACK_DMAS)
                    nc.gpsimd.tensor_tensor(k_lo[:, t % 2, :], c_in[:, t % 2, :], k_hi[:, t % 2, :].bitcast(F32),
                                            ALU.subtract).then_inc(k_lo_ready, 1)
                    upto(pool, q_hi_ready, t + 1, i, 2)
                    nc.gpsimd.tensor_tensor(q_lo[:, t % 2, :], x_in[:, t % 2, :], q_hi[:, t % 2, :].bitcast(F32),
                                            ALU.subtract).then_inc(q_lo_ready, 1)
                t = (s - 6) // 2
                if even and runs(t, i, TILES, 2):
                    inverse_deviation(moments2_ready, t + 1, i, 2 + t % 2, var2_ready, rstd2_ready)
                    if t == 0:
                        pool.wait_ge(small_loaded, 5 * DMA)
                    upto(pool, rstd2_ready, t + 1, i, 2)
                    nc.gpsimd.tensor_tensor(rstd[:, 2 + t % 2, :], rstd[:, 2 + t % 2, :], scalars[:, 3:4],
                                            ALU.mult).then_inc(rstd2_scaled, 1)
                    shift_of(rstd2_scaled, t + 1, i, 2 + t % 2, shift2_product, shift2_ready)
                t = (s - 7) // 2
                if not even and runs(t, i, TILES, 2):
                    m, zz = magic[:, t % 2, :], z[:, t % 2, :]
                    upto(pool, magic_ready, t + 1, i, 2)
                    nc.gpsimd.tensor_tensor(zz, zz, m, ALU.add).then_inc(rounded_up, 1)
                    upto(pool, rounded_up, t + 1, i, 2)
                    upto(pool, q8_t_ready, t - 1, i, 2)
                    nc.gpsimd.tensor_tensor(q8[:, t % 2, :], zz, m, ALU.subtract).then_inc(q8_ready, 1)
                t = (s + 5) // 2
                if not even and runs(t, i, TILES, 2):
                    inverse_deviation(moments_ready, t + 1, i, t % 2, var_ready, rstd_ready)
                    shift_of(rstd_ready, t + 1, i, t % 2, shift_product, shift_ready)
                if s == -2:
                    pool.wait_ge(q_lo_ready, 2)
                    nc.gpsimd.memset(k_stack[ONES_ROW:ONES_ROW + 1, :, :].bitcast(F32), 1.0
                                     ).then_inc(ones_row_ready, 1)
                    pool.wait_ge(ones_row_ready, 1)
                if s in (2, 3, 4, 5):
                    round_weights(s - 2)
                if s in (4, 5, 6, 7):
                    finish_weights(s - 4)
                t = (s - 5) // 2
                if not even and runs(t, i, TILES, 2):
                    upto(pool, o_saved, t + 1, i, 2)
                    upto(pool, inv_broadcast, DMA * (t + 1), i, 2 * DMA)
                    nc.gpsimd.tensor_tensor(o_sb[:, t % 2, :], o_sb[:, t % 2, :], inv_sb[:, t % 2, :],
                                            ALU.mult).then_inc(o_normed, 1)

            steps(pool, step)

        @block.scalar
        def _(act):

            def step(s, i):
                even = s % 2 == 0

                def free_attention_banks():
                    t = (s - 4) // 2
                    if even and runs(t, i, TILES, 2):
                        upto(act, pv_done, t + 1, i, 2)
                        upto(act, x1_ready, t - 1, i, 2)
                        nc.scalar.copy(o_sb[:, t % 2, :], ps_o[:]).then_inc(o_saved, 1)
                        upto(act, den_spread, DMA * t, i, 2 * DMA)
                        nc.scalar.copy(den_sb[:], ps_den[:]).then_inc(den_saved, 1)

                def save_max_rows():
                    n = s + 1
                    if runs(n, i, STEPS, BODY):
                        upto(act, max_t_ready, n + 1, i, BODY)
                        if i is not None or n >= 2:
                            upto(act, max_stacked[(n - 2) % BODY], DMA * ((n - 2) // BODY + 1), i, DMA)
                        nc.scalar.copy(max_rows[:, n % 2, :], ps_small[0:UNITS, 0:P]).then_inc(max_rows_ready, 1)

                def split_k():
                    t = (s + 5) // 2
                    if not even and runs(t, i, TILES, 2):
                        upto(act, c_loaded[t % 2], DMA * (t // 2 + 1), i, DMA)
                        for n in (2 * t - 4, 2 * t - 3):
                            upto(act, stacked[n % BODY], DMA * STACK_DMAS * (n // BODY + 1), i, DMA * STACK_DMAS)
                        nc.scalar.copy(k_hi[:, t % 2, :], c_in[:, t % 2, :]).then_inc(k_hi_ready, 1)

                def normalise_x():
                    t = (s + 4) // 2
                    if even and runs(t, i, TILES, 2):
                        upto(act, shift_ready, t + 1, i, 2)
                        nc.scalar.activation(x_in[:, t % 2, :], x_in[:, t % 2, :], ACT.Identity,
                                             scale=rstd[:, t % 2, :], bias=shift[:, t % 2, :]
                                             ).then_inc(q_normed, 1)

                def normalise_x1():
                    t = (s - 7) // 2
                    if not even and runs(t, i, TILES, 2):
                        upto(act, shift2_ready, t + 1, i, 2)
                        nc.scalar.activation(z[:, t % 2, :], x1[:, t % 2, :], ACT.Identity,
                                             scale=rstd[:, 2 + t % 2, :], bias=shift[:, 2 + t % 2, :]
                                             ).then_inc(z_ready, 1)

                def split_q():
                    t = (s + 4) // 2
                    if even and runs(t, i, TILES, 2):
                        upto(act, q_normed, t + 1, i, 2)
                        nc.scalar.copy(q_hi[:, t % 2, :], x_in[:, t % 2, :]).then_inc(q_hi_ready, 1)

                def save_v():
                    t = s // 2
                    if even and runs(t, i, TILES, 2):
                        upto(act, v_t_ready, t + 1, i, 2)
                        upto(act, pv_done, t - 1, i, 2)
                        nc.scalar.copy(v_t[:, t % 2, :, :], ps_small[:].rearrange("p (c r) -> p c r", c=CHUNKS)
                                       ).then_inc(v_t_saved, 1)

                def save_q8():
                    t = (s - 9) // 2
                    if not even and runs(t, i, TILES, 2):
                        upto(act, q8_t_ready, t + 1, i, 2)
                        nc.scalar.mul(q8_t[:, t % 2, :, :], ps_small.ap().bitcast(BF16)[:, 0:L].rearrange(
                            "p (c r) -> p c r", c=CHUNKS), FP16_GUARD).then_inc(q8_t_saved, 1)

                def exponentials(u):
                    if runs(s, i, STEPS, BODY):
                        upto(act, st_ready, UNITS * s + u + 1, i, UNITS * BODY)
                        t = s // 2
                        if u == 0:
                            upto(act, pv_done, t - 1, i, 2)
                        nc.scalar.activation(probs[:, t % 2, PAIR * (s % 2) + u // CHUNKS, u % CHUNKS, :],
                                             ps_st[u % 2][:], ACT.Exp, scale=SM_SCALE).then_inc(probs_ready, 1)

                free_attention_banks()
                exponentials(0)
                exponentials(1)
                save_max_rows()
                normalise_x()
                normalise_x1()
                exponentials(2)
                exponentials(3)
                split_q()
                save_q8()
                exponentials(4)
                exponentials(5)
                save_v()
                exponentials(6)
                exponentials(7)
                split_k()
                if s in (3, 4, 5, 6):
                    c = s - 3
                    act.wait_ge(w_rounded, c + 1)
                    nc.scalar.mul(w_nan[:, c, :], w_f[:, c, :], FP16_GUARD).then_inc(w_guarded, 1)
                if s == 0:
                    act.wait_ge(small_loaded, 5 * DMA)
                    nc.scalar.activation(gates[:], scalars[:, 0:2], ACT.Tanh).then_inc(gates_ready, 1)

            steps(act, step)

        @block.vector
        def _(dve):
            chain = [0]

            def link(ins):
                chain[0] += 1
                ins.then_inc(gates_chain, 1)
                dve.wait_ge(gates_chain, chain[0])

            def gains():
                dve.wait_ge(small_loaded, 5 * DMA)
                link(nc.vector.reciprocal(recips[:], scalars[:, 3:5]))
                dve.wait_ge(gates_ready, 1)
                nc.vector.tensor_scalar(att_gain[:], gates[:, 0:1], scalars[:, 2:3], None, ALU.mult)
                link(nc.vector.tensor_scalar(ffn_scale[:, 0:1], gates[:, 1:2], recips[:, 0:1], recips[:, 1:2],
                                             ALU.mult, ALU.mult))
                link(nc.vector.tensor_scalar(ffn_scale[:, 0:1], ffn_scale[:, 0:1], 1.0 / FP16_GUARD, None,
                                             ALU.mult))

            def round_weights(s):
                if s == 0:
                    dve.wait_ge(w_loaded, DMA)
                    dve.wait_ge(small_loaded, 5 * DMA)
                    nc.vector.tensor_scalar(w_f[:], w_f[:], scalars[:, 4:5], None, ALU.mult).then_inc(w_scaled, 1)
                if s == 1:
                    dve.wait_ge(w_scaled, 1)
                    nc.vector.tensor_scalar(w_magic[:].bitcast(U32), w_f[:].bitcast(U32), EXPONENT_BITS, None,
                                            ALU.bitwise_and).then_inc(w_exponent_ready, 1)
                if s == 2:
                    dve.wait_ge(w_exponent_ready, 1)
                    nc.vector.tensor_scalar(w_magic[:], w_magic[:], ROUND_AT, ROUND_LEAST, ALU.mult, ALU.max
                                            ).then_inc(w_magic_ready, 1)
                if s in (4, 5, 6, 7):
                    c = s - 4
                    dve.wait_ge(w_guarded, c + 1)
                    nc.vector.tensor_tensor(w_nan[:, c, :], w_nan[:, c, :], w_nan[:, c, :], ALU.subtract
                                            ).then_inc(w_nan_ready, 1)

            def step(s, i):
                even = s % 2 == 0

                def maximum(u):
                    n = s + 2
                    if runs(n, i, STEPS, BODY):
                        upto(dve, s_ready, UNITS * n + u + 1, i, UNITS * BODY)
                        if u == 0:
                            upto(dve, max_t_ready, n - 1, i, BODY)
                        nc.vector.tensor_reduce(neg_max[:, n % 2, u:u + 1], ps_s[u % 2][:], AX, ALU.max,
                                                negate=True).then_inc(maxed, 1)

                def sum_pair(j):
                    n = s - 1
                    if runs(n, i, STEPS, BODY):
                        t = n // 2
                        upto(dve, probs_ready, UNITS * n + CHUNKS * j + 2, i, UNITS * BODY)
                        upto(dve, pv_done, t - 1, i, 2)
                        h = PAIR * (n % 2) + j
                        nc.vector.tensor_tensor(pair_sums[:, t % 2, h, :], probs[:, t % 2, h, 0, :],
                                                probs[:, t % 2, h, 1, :], ALU.add).then_inc(pairs_summed, 1)

                def measure_x():
                    t = (s + 5) // 2
                    if not even and runs(t, i, TILES, 2):
                        upto(dve, x_loaded[t % 2], DMA * (t // 2 + 1), i, DMA)
                        nc.vector.bn_stats(stats[:, t % 2, :], x_in[:, t % 2, :]).then_inc(stats_ready, 1)
                        upto(dve, stats_ready, t + 1, i, 2)

                def moments_of_x():
                    t = (s + 5) // 2
                    if not even and runs(t, i, TILES, 2):
                        nc.vector.bn_aggr(moments[:, t % 2, :], stats[:, t % 2, :]).then_inc(moments_ready, 1)

                def invert_sums():
                    t = (s - 5) // 2
                    if not even and runs(t, i, TILES, 2):
                        upto(dve, den_spread, DMA * (t + 1), i, 2 * DMA)
                        nc.vector.reciprocal(den_col[:, t % 2, :], den_col[:, t % 2, :]).then_inc(sums_inverted, 1)
                        upto(dve, sums_inverted, t + 1, i, 2)
                        nc.vector.tensor_scalar(den_col[:, t % 2, :], den_col[:, t % 2, :], att_gain[:], None,
                                                ALU.mult).then_inc(inv_ready, 1)

                def measure_x1():
                    t = (s - 6) // 2
                    if even and runs(t, i, TILES, 2):
                        upto(dve, x1_ready, t + 1, i, 2)
                        nc.vector.bn_stats(stats[:, 2 + t % 2, :], x1[:, t % 2, :]).then_inc(stats2_ready, 1)
                        upto(dve, stats2_ready, t + 1, i, 2)

                def moments_of_x1():
                    t = (s - 6) // 2
                    if even and runs(t, i, TILES, 2):
                        nc.vector.bn_aggr(moments[:, 2 + t % 2, :], stats[:, 2 + t % 2, :]
                                          ).then_inc(moments2_ready, 1)

                def powers_of_two():
                    t = (s - 7) // 2
                    if not even and runs(t, i, TILES, 2):
                        upto(dve, z_ready, t + 1, i, 2)
                        nc.vector.tensor_scalar(magic[:, t % 2, :].bitcast(U32), z[:, t % 2, :].bitcast(U32),
                                                EXPONENT_BITS, None, ALU.bitwise_and).then_inc(exponent_ready, 1)

                def magic_numbers():
                    t = (s - 7) // 2
                    if not even and runs(t, i, TILES, 2):
                        upto(dve, exponent_ready, t + 1, i, 2)
                        nc.vector.tensor_scalar(magic[:, t % 2, :], magic[:, t % 2, :], ROUND_AT, ROUND_LEAST,
                                                ALU.mult, ALU.max).then_inc(magic_ready, 1)

                def gain_of_rows():
                    t = (s - 9) // 2
                    if not even and runs(t, i, TILES, 2):
                        upto(dve, nan_ready, t + 1, i, 2)
                        nc.vector.tensor_scalar(ffn_gain[:, t % 2, :], ps_small[:, 0:1], ffn_scale[:, 0:1], None,
                                                ALU.add).then_inc(gain_ready, 1)

                def add_product():
                    t = (s - 10) // 2
                    if even and runs(t, i, TILES, 2):
                        upto(dve, y_ready, t + 1, i, 2)
                        upto(dve, gain_ready, t + 1, i, 2)
                        upto(dve, y_sb_free[t % 2], DMA * (t // 2 + 1), i, DMA)
                        nc.vector.scalar_tensor_tensor(out=y_sb[:, t % 2, :], in0=ps_y[:], scalar=ffn_gain[:, t % 2, :],
                                                       in1=x1[:, t % 2, :], op0=ALU.mult,
                                                       op1=ALU.add).then_inc(y_added, 1)

                maximum(0)
                maximum(1)
                add_product()
                invert_sums()
                if not even:
                    sum_pair(0)
                maximum(2)
                maximum(3)
                if even:
                    sum_pair(0)
                round_weights(s)
                powers_of_two()
                maximum(4)
                maximum(5)
                measure_x1()
                magic_numbers()
                measure_x()
                maximum(6)
                moments_of_x1()
                moments_of_x()
                maximum(7)
                gain_of_rows()
                sum_pair(1)
                if s == -2:
                    dve.wait_ge(constants_ready, CONSTANTS)
                    nc.vector.tensor_copy(ident16[:], ident[:]).then_inc(ident16_ready, 1)
                if s == 1:
                    gains()

            steps(dve, step)

        @block.tensor
        def _(pe):
            pe.wait_ge(constants_ready, CONSTANTS)

            def step(s, i):
                even = s % 2 == 0

                def scores_t(u):
                    if runs(s, i, STEPS, BODY):
                        slot, c = PAIR * (s % BODY) + u // CHUNKS, u % CHUNKS
                        if s == 0 and u == 0:
                            pe.wait_ge(ones_row_ready, 1)
                        if u == 0:
                            upto(pe, max_stacked[s % BODY], DMA * (s // BODY + 1), i, DMA)
                        upto(pe, probs_ready, UNITS * s + u - 1, i, UNITS * BODY)
                        nc.tensor.matmul(ps_st[u % 2][:], k_stack[0:ONES_ROW + 1, slot, c * P:(c + 1) * P],
                                         q_stack[0:ONES_ROW + 1, slot, :], start=True, stop=True
                                         ).then_inc(st_ready, 1)

                def scores(u):
                    n = s + 2
                    if runs(n, i, STEPS, BODY):
                        slot, c = PAIR * (n % BODY) + u // CHUNKS, u % CHUNKS
                        if u == 0:
                            upto(pe, stacked[n % BODY], DMA * STACK_DMAS * (n // BODY + 1), i, DMA * STACK_DMAS)
                        upto(pe, maxed, UNITS * n + u - 1, i, UNITS * BODY)
                        nc.tensor.matmul(ps_s[u % 2][:], q_stack[0:ONES_ROW, slot, c * P:(c + 1) * P],
                                         k_stack[0:ONES_ROW, slot, :], start=True, stop=True).then_inc(s_ready, 1)

                def attend(g):
                    t = (s - 2) // 2
                    if not runs(t, i, TILES, 2):
                        return

                    def weigh(c):
                        for h in range(HEADS_PER_TILE):
                            rows = slice(D * h, D * h + D)
                            last = nc.tensor.matmul(ps_o[rows, :], v_t[:, t % 2, c, rows],
                                                    probs[:, t % 2, h, c, :], start=c == 0, stop=c == CHUNKS - 1)
                        return last

                    def add_up(moving, start, stop):
                        for h in range(HEADS_PER_TILE):
                            nc.tensor.matmul(ps_den[D * h:D * h + D, :], ones[:], moving[:, h, :],
                                             start=start, stop=stop)

                    if even and g == 0:
                        upto(pe, probs_ready, 2 * UNITS * (t + 1) - CHUNKS + 1, i, 4 * UNITS)
                        upto(pe, v_t_saved, t + 1, i, 2)
                        upto(pe, o_saved, t, i, 2)
                        weigh(0)
                    elif even and g == 1:
                        upto(pe, probs_ready, 2 * UNITS * (t + 1) - CHUNKS + 2, i, 4 * UNITS)
                        weigh(1)
                    elif even and g == 2:
                        upto(pe, probs_ready, 2 * UNITS * (t + 1) - CHUNKS + 3, i, 4 * UNITS)
                        upto(pe, den_saved, t, i, 2)
                        add_up(probs[:, t % 2, :, 2, :], True, False)
                    elif even and g == 3:
                        upto(pe, probs_ready, 2 * UNITS * (t + 1), i, 4 * UNITS)
                        add_up(probs[:, t % 2, :, 3, :], False, False)
                    elif g == 0:
                        weigh(2)
                    elif g == 1:
                        upto(pe, pairs_summed, HEADS_PER_TILE * (t + 1), i, 2 * HEADS_PER_TILE)
                        add_up(pair_sums[:, t % 2, :, :], False, True)
                    elif g == 3:
                        weigh(3).then_inc(pv_done, 1)

                def transpose_max():
                    n = s + 1
                    if runs(n, i, STEPS, BODY):
                        upto(pe, maxed, UNITS * (n + 1), i, UNITS * BODY)
                        upto(pe, max_rows_ready, n, i, BODY)
                        if even:
                            upto(pe, gain_ready, (s - 10) // 2 + 1, i, 2)
                        else:
                            upto(pe, v_t_saved, (s - 1) // 2 + 1, i, 2)
                        nc.tensor.transpose(ps_small[0:UNITS, 0:P], neg_max[:, n % 2, :], ident[:]
                                            ).then_inc(max_t_ready, 1)

                def transpose_v():
                    t = s // 2
                    if even and runs(t, i, TILES, 2):
                        upto(pe, v_loaded, DMA * (t + 1), i, 2 * DMA)
                        upto(pe, max_rows_ready, s + 2, i, BODY)
                        for c in range(CHUNKS):
                            last = nc.tensor.transpose(ps_small[:, c * P:(c + 1) * P],
                                                       v_in[:, c * P:(c + 1) * P], ident[:])
                        last.then_inc(v_t_ready, 1)

                def transpose_q8():
                    t = (s - 9) // 2
                    if not even and runs(t, i, TILES, 2):
                        upto(pe, q8_ready, t + 1, i, 2)
                        upto(pe, max_rows_ready, min(s + 2, STEPS) if i is None else s + 2, i, BODY)
                        upto(pe, v_t_saved, min((s - 1) // 2 + 1, TILES) if i is None else (s - 1) // 2 + 1, i, 2)
                        upto(pe, gain_ready, t, i, 2)
                        if t == 0:
                            pe.wait_ge(ident16_ready, 1)
                        for c in range(CHUNKS):
                            last = nc.tensor.transpose(ps_small.ap().bitcast(BF16)[:, c * P:(c + 1) * P],
                                                       q8[:, t % 2, c * P:(c + 1) * P], ident16[:])
                        last.then_inc(q8_t_ready, 1)

                def product():
                    t = (s - 9) // 2
                    if not even and runs(t, i, TILES, 2):
                        upto(pe, q8_t_saved, t + 1, i, 2)
                        upto(pe, y_added, t, i, 2)
                        if t == 0:
                            pe.wait_ge(weights_ready, CHUNKS)
                        for c in range(CHUNKS):
                            last = nc.tensor.matmul(ps_small[:, 0:1], q8_t[:, t % 2, c, :], zero16[:],
                                                    start=c == 0, stop=c == CHUNKS - 1)
                        last.then_inc(nan_ready, 1)
                        for c in range(CHUNKS):
                            last = nc.tensor.matmul(ps_y[:], q8_t[:, t % 2, c, :], w8[:, c, :],
                                                    start=c == 0, stop=c == CHUNKS - 1)
                        last.then_inc(y_ready, 1)

                for u in range(UNITS):
                    scores_t(u)
                    scores(u)
                    if u % 2 == 1:
                        attend(u // 2)
                    if u == 1:
                        transpose_max()
                    if u == 3:
                        transpose_v()
                        transpose_q8()
                    if u == 5:
                        product()

            steps(pe, step)


_INS = ["x", "ctx_2048", "g_xattn", "g_ffn", "L0_xattn_gamma", "L0_ffn_input2", "L0_ffn_scale", "L0_ffn_scale1"]


def kernel(**inputs):
    import numpy as _np
    import concourse.bacc as _bacc
    from concourse import mybir as _mybir
    from concourse.bass_utils import run_bass_kernel_spmd as _run

    nc = _bacc.Bacc("TRN2", target_bir_lowering=False, num_devices=1)
    arrays, args = {}, []
    for name in _INS:
        a = _np.ascontiguousarray(inputs[name])
        arrays[f"in_{name}"] = a
        args.append(nc.dram_tensor(f"in_{name}", a.shape, _mybir.dt.from_np(a.dtype), kind="ExternalInput").ap())
    args.append(nc.dram_tensor("out_x", (IMAGES, CHANNELS, L), F32, kind="ExternalOutput").ap())
    build(nc, *args)
    r = _run(nc, [arrays], core_ids=[0])
    return r.results[0]["out_x"]
```

```python
from contextlib import ExitStack

import concourse.bass as bass
from concourse import mybir

F32 = mybir.dt.float32
F32R = mybir.dt.float32r
BF16 = mybir.dt.bfloat16
F16 = mybir.dt.float16
U32 = mybir.dt.uint32
ALU = mybir.AluOpType
ACT = mybir.ActivationFunctionType
AX = mybir.AxisListType.X

P = 128
L = 512
D = 32
IMAGES, CHANNELS = 8, 256
TILES = IMAGES * CHANNELS // P
HEADS_PER_TILE = P // D
PAIR = 2
STEPS = TILES * HEADS_PER_TILE // PAIR
CHUNKS = L // P
UNITS = PAIR * CHUNKS
SLOTS = 2 * HEADS_PER_TILE
ONES_ROW = 3 * D
Q_HI, Q_LO, K_HI, K_LO = range(4)
STACKED = ((Q_HI, K_HI), (Q_LO, K_HI), (Q_HI, K_LO))
STACK_DMAS = len(STACKED)
LN_EPS = 1e-5
SM_SCALE = float(D) ** -0.5
CONSTANTS = 6
DMA = 16

EXPONENT_BITS = 0x7F800000
ROUND_AT = 1.5 * 2.0 ** 20
ROUND_LEAST = ROUND_AT * 2.0 ** -6
FP16_GUARD = 144.0

FIRST_STEP, LOOP_FIRST, LOOPS, LAST_STEP = -6, 10, 4, STEPS + 10
BODY = 4
LAST = TILES - 1
FIRST_ROUNDED_BY_DVE = TILES - 3


def upto(eng, sem, count, i, per_loop):
    if i is None:
        if count > 0:
            eng.wait_ge(sem, count)
    else:
        assert count > 0
        eng.wait_ge(sem, i * per_loop + count)


def runs(index, i, n, per_loop):
    if i is None:
        return 0 <= index < n
    assert index >= 0 and index + per_loop * (LOOPS - 1) < n
    return True


def is_last(t, i):
    return i is None and t == LAST


def in_place(t, i):
    return i is None and t >= LAST - 1


def is_first(t, i):
    return i is None and t == 0


def rounded_by_dve(t, i):
    return i is None and t >= FIRST_ROUNDED_BY_DVE


def steps(eng, step):
    for s in range(FIRST_STEP, LOOP_FIRST):
        step(s, None)
    with eng.Fori(0, LOOPS) as i:
        for s in range(LOOP_FIRST, LOOP_FIRST + BODY):
            step(s, i)
    for s in range(LOOP_FIRST + BODY * LOOPS, LAST_STEP):
        step(s, None)


def build(nc, x, ctx_in, g_xattn, g_ffn, gamma, w_in, scale_in, scale1_in, out):
    x_t = x.rearrange("b c l -> (b c) l").rearrange("(t p) l -> t p l", p=P)
    c_t = ctx_in.rearrange("b c l -> (b c) l").rearrange("(t p) l -> t p l", p=P)
    out_t = out.rearrange("b c l -> (b c) l").rearrange("(t p) l -> t p l", p=P)
    w_k = w_in.rearrange("(k p) n -> p k n", p=P)

    def tile_of(dram, t, i):
        return dram[t, :, :] if i is None else dram[bass.ds(i * 2 + t, 1), :, :].rearrange("a p l -> (a p) l")

    es = ExitStack()
    with es:
        def sb(name, shape, dt=F32):
            return es.enter_context(nc.sbuf_tensor(name, shape, dt))

        def pb(name):
            return es.enter_context(nc.psum_tensor(name, [P, L], F32))

        def sem(name):
            return es.enter_context(nc.semaphore(name))

        stack = sb("stack", [P, 2, SLOTS, L], F32R)
        q_stack, k_stack = stack[:, 0, :, :], stack[:, 1, :, :]
        probs = sb("probs", [P, 2, HEADS_PER_TILE, CHUNKS, L])
        pair_sums = sb("pair_sums", [P, 2, HEADS_PER_TILE, L])
        x_in = sb("x_in", [P, 2, L])
        c_in = sb("c_in", [P, 2, L])
        halves = sb("halves", [P, 2, 4, L], F32R)
        q_hi, q_lo, k_hi, k_lo = (halves[:, :, n, :] for n in (Q_HI, Q_LO, K_HI, K_LO))
        v_in = sb("v_in", [P, L])
        v_t = sb("v_t", [P, 2, CHUNKS, P])
        o_sb = sb("o_sb", [P, 2, L])
        den_sb = sb("den_sb", [P, L])
        inv_rows = sb("inv_rows", [HEADS_PER_TILE, 2, L])
        inv_sb = sb("inv_sb", [P, 2, L])
        x_res = sb("x_res", [P, 2, L])
        x1 = sb("x1", [P, 2, L])
        z = sb("z", [P, 2, L])
        magic = sb("magic", [P, 2, L])
        q8 = sb("q8", [P, 2, L], BF16)
        q8_t = sb("q8_t", [P, 2, CHUNKS, P], F16)
        y_sb = sb("y_sb", [P, 2, L])
        den_col = sb("den_col", [P, 2, L * HEADS_PER_TILE // P])
        neg_max = sb("neg_max", [P, 2, UNITS])
        max_rows = sb("max_rows", [UNITS, 2, P])
        stats = sb("stats", [P, 4, nc.vector.BN_STATS_DIM])
        moments = sb("moments", [P, 4, 2])
        rstd = sb("rstd", [P, 4, 1])
        shift = sb("shift", [P, 4, 1])
        zero = sb("zero", [P, 1])
        zero16 = sb("zero16", [P, 1], BF16)
        minus_half = sb("minus_half", [P, 1])
        eps = sb("eps", [P, 1])
        ffn_gain = sb("ffn_gain", [P, 2, 1])
        scalars = sb("scalars", [P, 5])
        gates = sb("gates", [P, 2])
        recips = sb("recips", [P, 2])
        att_gain = sb("att_gain", [P, 1])
        ffn_scale = sb("ffn_scale", [P, 1])
        w_f = sb("w_f", [P, CHUNKS, L])
        w_magic = sb("w_magic", [P, CHUNKS, L])
        w_nan = sb("w_nan", [P, CHUNKS, L], F16)
        w8 = sb("w8", [P, CHUNKS, L], BF16)
        ident = sb("ident", [P, P])
        ident16 = sb("ident16", [P, P], BF16)
        ones = sb("ones", [P, D])

        ps_st = [pb(f"ps_st{n}") for n in range(2)]
        ps_s = [pb(f"ps_s{n}") for n in range(2)]
        ps_o = pb("ps_o")
        ps_den = pb("ps_den")
        ps_small = pb("ps_small")
        ps_y = pb("ps_y")

        def x1_of(t, i):
            return x_res[:, t % 2, :] if in_place(t, i) else x1[:, t % 2, :]

        def s_bank(s, u):
            return (*ps_s, ps_o, ps_den)[u % 4] if s < 0 else ps_s[u % 2]

        def stacks_copied(eng, t, i):
            for h in range(HEADS_PER_TILE):
                slot = (HEADS_PER_TILE * t + h) % SLOTS
                upto(eng, stacked[slot], DMA * STACK_DMAS * (t // 2 + 1), i, DMA * STACK_DMAS)

        x_loaded = [sem(f"x_loaded{n}") for n in range(2)]
        c_loaded = [sem(f"c_loaded{n}") for n in range(2)]
        v_loaded = sem("v_loaded")
        res_loaded = [sem(f"res_loaded{n}") for n in range(2)]
        stacked = [sem(f"stacked{n}") for n in range(SLOTS)]
        max_stacked = [sem(f"max_stacked{n}") for n in range(BODY)]
        den_spread = sem("den_spread")
        inv_gathered = sem("inv_gathered")
        inv_broadcast = sem("inv_broadcast")
        y_sb_free = [sem(f"y_sb_free{n}") for n in range(2)]
        small_loaded = sem("small_loaded")
        w_loaded = sem("w_loaded")
        st_ready = sem("st_ready")
        s_ready = sem("s_ready")
        max_t_ready = sem("max_t_ready")
        v_t_ready = sem("v_t_ready")
        pv_done = sem("pv_done")
        sums_done = sem("sums_done")
        q8_t_ready = sem("q8_t_ready")
        nan_ready = sem("nan_ready")
        y_ready = sem("y_ready")
        probs_ready = sem("probs_ready")
        max_rows_ready = sem("max_rows_ready")
        v_t_saved = sem("v_t_saved")
        q8_t_saved = sem("q8_t_saved")
        o_saved = sem("o_saved")
        den_saved = sem("den_saved")
        k_hi_ready = sem("k_hi_ready")
        q_normed = sem("q_normed")
        q_hi_ready = sem("q_hi_ready")
        z_ready = sem("z_ready")
        gates_ready = sem("gates_ready")
        w_scaled = sem("w_scaled")
        w_guarded = sem("w_guarded")
        maxed = sem("maxed")
        pairs_summed = sem("pairs_summed")
        stats_ready = sem("stats_ready")
        moments_ready = sem("moments_ready")
        inv_ready = sem("inv_ready")
        last_inverted = sem("last_inverted")
        last_normed = sem("last_normed")
        stats2_ready = sem("stats2_ready")
        moments2_ready = sem("moments2_ready")
        exponent_ready = sem("exponent_ready")
        magic_ready = sem("magic_ready")
        sums_inverted = sem("sums_inverted")
        gain_ready = sem("gain_ready")
        y_added = sem("y_added")
        gates_chain = sem("gates_chain")
        w_exponent_ready = sem("w_exponent_ready")
        w_magic_ready = sem("w_magic_ready")
        w_nan_ready = sem("w_nan_ready")
        ident16_ready = sem("ident16_ready")
        weights_ready = sem("weights_ready")
        w_rounded_up = sem("w_rounded_up")
        w_rounded = sem("w_rounded")
        constants_ready = sem("constants_ready")
        ones_row_ready = sem("ones_row_ready")
        ident_zeroed = sem("ident_zeroed")
        rstd_ready = sem("rstd_ready")
        rstd2_ready = sem("rstd2_ready")
        rstd2_scaled = sem("rstd2_scaled")
        shift_product = sem("shift_product")
        shift_ready = sem("shift_ready")
        shift2_product = sem("shift2_product")
        shift2_ready = sem("shift2_ready")
        k_lo_ready = sem("k_lo_ready")
        q_lo_ready = sem("q_lo_ready")
        o_normed = sem("o_normed")
        x1_ready = sem("x1_ready")
        rounded_up = sem("rounded_up")
        q8_ready = sem("q8_ready")
        var_ready = sem("var_ready")
        var2_ready = sem("var2_ready")

        half_ready = {Q_HI: q_hi_ready, Q_LO: q_lo_ready, K_HI: k_hi_ready, K_LO: k_lo_ready}

        block = es.enter_context(nc.Block())

        @block.sync
        def _(sp):
            def step(s, i):
                even = s % 2 == 0

                def stack_head(j):
                    n = s + 3
                    if runs(n, i, STEPS, BODY):
                        t = n // 2
                        upto(sp, st_ready, UNITS * (n - 4) + CHUNKS * (j + 1), i, UNITS * BODY)
                        row = D * (PAIR * (n % 2) + j)
                        slot = PAIR * (n % BODY) + j
                        for place, (q_part, k_part) in enumerate(STACKED):
                            both = slice(q_part, k_part + 1, k_part - q_part)
                            for part in (q_part, k_part):
                                upto(sp, half_ready[part], t + 1, i, 2)
                            sp.dma_start(stack[D * place:D * place + D, :, slot, :].bitcast(F32),
                                         halves[row:row + D, t % 2, both, :].bitcast(F32)
                                         ).then_inc(stacked[slot], DMA)

                def stack_max():
                    n = s + 1
                    if runs(n, i, STEPS, BODY):
                        upto(sp, max_rows_ready, n + 1, i, BODY)
                        slot = PAIR * (n % BODY)
                        sp.dma_start(q_stack[ONES_ROW:ONES_ROW + 1, slot:slot + PAIR, :].bitcast(F32),
                                     max_rows[:, n % 2, :]).then_inc(max_stacked[n % BODY], DMA)

                def spread_sums():
                    t = (s - 4) // 2
                    if even and runs(t, i, TILES, 2) and not is_last(t, i):
                        upto(sp, den_saved, t + 1, i, 2)
                        sp.dma_start(den_col[:, t % 2, :], den_sb[0:P:D, :]).then_inc(den_spread, DMA)

                def gather_sums():
                    t = (s - 5) // 2
                    if not even and runs(t, i, TILES, 2) and not is_last(t, i):
                        upto(sp, inv_ready, t + 1, i, 2)
                        sp.dma_start(inv_rows[:, t % 2, :], den_col[:, t % 2, :]).then_inc(inv_gathered, DMA)

                def broadcast_sums():
                    t = (s - 5) // 2
                    if not even and runs(t, i, TILES, 2) and not is_last(t, i):
                        upto(sp, inv_gathered, DMA * (t + 1), i, 2 * DMA)
                        upto(sp, o_normed, t - 1, i, 2)
                        sp.dma_start(inv_sb[:, t % 2, :], inv_rows[:, t % 2, :].unsqueeze(1).to_broadcast(
                            [HEADS_PER_TILE, D, L])).then_inc(inv_broadcast, DMA)

                def load():
                    t = (s + 6) // 2
                    if even and (i is None or t < TILES) and runs(t, i, TILES, 2):
                        upto(sp, q_lo_ready, t - 1, i, 2)
                        sp.dma_start(x_in[:, t % 2, :], tile_of(x_t, t, i)).then_inc(x_loaded[t % 2], DMA)
                        upto(sp, k_hi_ready, t - 1, i, 2)
                        upto(sp, k_lo_ready, t - 1, i, 2)
                        sp.dma_start(c_in[:, t % 2, :], tile_of(c_t, t, i)).then_inc(c_loaded[t % 2], DMA)

                def load_v():
                    t = (s + 1) // 2
                    if not even and runs(t, i, TILES, 2):
                        upto(sp, v_t_ready, t, i, 2)
                        sp.dma_start(v_in[:], tile_of(c_t, t, i)).then_inc(v_loaded, DMA)

                def load_residual():
                    t = (s - 4) // 2
                    if even and runs(t, i, TILES, 2):
                        upto(sp, x1_ready, t - 1, i, 2)
                        sp.dma_start(x_res[:, t % 2, :], tile_of(x_t, t, i)).then_inc(res_loaded[t % 2], DMA)

                def store():
                    t = (s - 10) // 2
                    if even and runs(t, i, TILES, 2):
                        upto(sp, y_added, t + 1, i, 2)
                        sp.dma_start(tile_of(out_t, t, i), y_sb[:, t % 2, :]).then_inc(y_sb_free[t % 2], DMA)

                stack_head(0)
                stack_max()
                spread_sums()
                gather_sums()
                stack_head(1)
                broadcast_sums()
                load()
                load_v()
                load_residual()
                store()

            steps(sp, step)
            for n in range(2):
                sp.wait_ge(y_sb_free[n], DMA * (TILES // 2 + 1))

        @block.gpsimd
        def _(pool):
            nc.gpsimd.memset(minus_half[:], -0.5).then_inc(constants_ready, 1)
            nc.gpsimd.memset(zero[:], 0.0).then_inc(constants_ready, 1)
            nc.gpsimd.memset(eps[:], LN_EPS).then_inc(constants_ready, 1)
            pool.wait_ge(constants_ready, 3)

            def constants():
                nc.gpsimd.memset(ones[:], 1.0).then_inc(constants_ready, 1)
                nc.gpsimd.memset(zero16[:], 0.0).then_inc(constants_ready, 1)
                nc.gpsimd.memset(ident[:], 0.0).then_inc(ident_zeroed, 1)
                pool.wait_ge(ident_zeroed, 1)
                nc.gpsimd.affine_select(out=ident[:], in_=ident[:], compare_op=ALU.not_equal, fill=1.0, base=0,
                                        pattern=[[-1, P]], channel_multiplier=1).then_inc(constants_ready, 1)
                for n in range(2):
                    nc.gpsimd.memset(y_sb[:, n, 0:1], 0.0).then_inc(y_sb_free[n], DMA)

            def round_weights(c):
                w, m = w_f[:, c, :], w_magic[:, c, :]
                pool.wait_ge(w_magic_ready, c + 1)
                nc.gpsimd.tensor_tensor(w, w, m, ALU.add).then_inc(w_rounded_up, 1)
                pool.wait_ge(w_rounded_up, c + 1)
                nc.gpsimd.tensor_tensor(w, w, m, ALU.subtract).then_inc(w_rounded, 1)

            def finish_weights(c):
                pool.wait_ge(w_nan_ready, c + 1)
                nc.gpsimd.tensor_tensor(w8[:, c, :], w_f[:, c, :], w_nan[:, c, :], ALU.add
                                        ).then_inc(weights_ready, 1)

            def inverse_deviation(measured, count, i, n, var_sem, done):
                upto(pool, measured, count, i, 2)
                nc.gpsimd.tensor_tensor(rstd[:, n, :], moments[:, n, 1:2], eps[:], ALU.add).then_inc(var_sem, 1)
                upto(pool, var_sem, count, i, 2)
                nc.gpsimd.tensor_tensor(rstd[:, n, :], rstd[:, n, :], minus_half[:], ALU.pow).then_inc(done, 1)

            def shift_of(scaled, count, i, n, product_sem, done):
                upto(pool, scaled, count, i, 2)
                nc.gpsimd.tensor_tensor(shift[:, n, :], moments[:, n, 0:1], rstd[:, n, :], ALU.mult
                                        ).then_inc(product_sem, 1)
                upto(pool, product_sem, count, i, 2)
                nc.gpsimd.tensor_tensor(shift[:, n, :], zero[:], shift[:, n, :], ALU.subtract).then_inc(done, 1)

            def step(s, i):
                even = s % 2 == 0
                if s == FIRST_STEP + 2:
                    constants()
                t = (s - 6) // 2
                if even and runs(t, i, TILES, 2) and not is_last(t, i):
                    upto(pool, o_normed, t + 1, i, 2)
                    if not in_place(t, i):
                        upto(pool, y_added, t - 1, i, 2)
                    upto(pool, res_loaded[t % 2], DMA * (t // 2 + 1), i, DMA)
                    nc.gpsimd.tensor_tensor(x1_of(t, i), o_sb[:, t % 2, :], x_res[:, t % 2, :],
                                            ALU.add).then_inc(x1_ready, 1)
                t = (s + 4) // 2
                if even and runs(t, i, TILES, 2) and not is_first(t, i):
                    upto(pool, k_hi_ready, t + 1, i, 2)
                    stacks_copied(pool, t - 2, i)
                    nc.gpsimd.tensor_tensor(k_lo[:, t % 2, :], c_in[:, t % 2, :], k_hi[:, t % 2, :].bitcast(F32),
                                            ALU.subtract).then_inc(k_lo_ready, 1)
                    upto(pool, q_hi_ready, t + 1, i, 2)
                    nc.gpsimd.tensor_tensor(q_lo[:, t % 2, :], x_in[:, t % 2, :], q_hi[:, t % 2, :].bitcast(F32),
                                            ALU.subtract).then_inc(q_lo_ready, 1)
                t = (s - 6) // 2
                if even and runs(t, i, TILES, 2):
                    inverse_deviation(moments2_ready, t + 1, i, 2 + t % 2, var2_ready, rstd2_ready)
                    if t == 0:
                        pool.wait_ge(small_loaded, 5 * DMA)
                    upto(pool, rstd2_ready, t + 1, i, 2)
                    nc.gpsimd.tensor_tensor(rstd[:, 2 + t % 2, :], rstd[:, 2 + t % 2, :], scalars[:, 3:4],
                                            ALU.mult).then_inc(rstd2_scaled, 1)
                    shift_of(rstd2_scaled, t + 1, i, 2 + t % 2, shift2_product, shift2_ready)
                t = (s - 7) // 2
                if not even and runs(t, i, TILES, 2) and not rounded_by_dve(t, i):
                    m, zz = magic[:, t % 2, :], z[:, t % 2, :]
                    upto(pool, magic_ready, t + 1, i, 2)
                    nc.gpsimd.tensor_tensor(zz, zz, m, ALU.add).then_inc(rounded_up, 1)
                    upto(pool, rounded_up, t + 1, i, 2)
                    upto(pool, q8_t_ready, t - 1, i, 2)
                    nc.gpsimd.tensor_tensor(q8[:, t % 2, :], zz, m, ALU.subtract).then_inc(q8_ready, 1)
                t = (s + 5) // 2
                if not even and runs(t, i, TILES, 2):
                    inverse_deviation(moments_ready, t + 1, i, t % 2, var_ready, rstd_ready)
                    shift_of(rstd_ready, t + 1, i, t % 2, shift_product, shift_ready)
                if s == -2:
                    pool.dma_start(w_f[:, :, :], w_k).then_inc(w_loaded, DMA)
                    for n, src in enumerate((g_xattn, g_ffn, gamma, scale_in, scale1_in)):
                        pool.dma_start(scalars[:, n:n + 1], src.unsqueeze(0).to_broadcast([P, 1])
                                       ).then_inc(small_loaded, DMA)
                    pool.wait_ge(q_lo_ready, 2)
                    nc.gpsimd.memset(k_stack[ONES_ROW:ONES_ROW + 1, :, :].bitcast(F32), 1.0
                                     ).then_inc(ones_row_ready, 1)
                    pool.wait_ge(ones_row_ready, 1)
                if s in (1, 2, 3, 4):
                    round_weights(s - 1)
                if s in (3, 4, 5, 6):
                    finish_weights(s - 3)
                t = (s - 5) // 2
                if not even and runs(t, i, TILES, 2) and not is_last(t, i):
                    upto(pool, o_saved, t + 1, i, 2)
                    upto(pool, inv_broadcast, DMA * (t + 1), i, 2 * DMA)
                    nc.gpsimd.tensor_tensor(o_sb[:, t % 2, :], o_sb[:, t % 2, :], inv_sb[:, t % 2, :],
                                            ALU.mult).then_inc(o_normed, 1)

            steps(pool, step)

        @block.scalar
        def _(act):

            def step(s, i):
                even = s % 2 == 0

                def save_attention():
                    t = (s - 4) // 2
                    if even and runs(t, i, TILES, 2):
                        upto(act, pv_done, t + 1, i, 2)
                        upto(act, x1_ready, t - 1, i, 2)
                        nc.scalar.copy(o_sb[:, t % 2, :], ps_o[:]).then_inc(o_saved, 1)

                def save_sums():
                    t = (s - 3) // 2
                    if not even and runs(t, i, TILES, 2):
                        upto(act, sums_done, t + 1, i, 2)
                        upto(act, den_spread, DMA * t, i, 2 * DMA)
                        nc.scalar.copy(den_sb[:], ps_den[:]).then_inc(den_saved, 1)

                def save_max_rows():
                    n = s + 1
                    if runs(n, i, STEPS, BODY):
                        upto(act, max_t_ready, n + 1, i, BODY)
                        if i is not None or n >= 2:
                            upto(act, max_stacked[(n - 2) % BODY], DMA * ((n - 2) // BODY + 1), i, DMA)
                        nc.scalar.copy(max_rows[:, n % 2, :], ps_small[0:UNITS, 0:P]).then_inc(max_rows_ready, 1)

                def split_k():
                    t = (s + 5) // 2
                    if not even and runs(t, i, TILES, 2):
                        upto(act, c_loaded[t % 2], DMA * (t // 2 + 1), i, DMA)
                        stacks_copied(act, t - 2, i)
                        nc.scalar.copy(k_hi[:, t % 2, :], c_in[:, t % 2, :]).then_inc(k_hi_ready, 1)

                def normalise_x():
                    t = (s + 4) // 2
                    if even and runs(t, i, TILES, 2):
                        upto(act, shift_ready, t + 1, i, 2)
                        nc.scalar.activation(x_in[:, t % 2, :], x_in[:, t % 2, :], ACT.Identity,
                                             scale=rstd[:, t % 2, :], bias=shift[:, t % 2, :]
                                             ).then_inc(q_normed, 1)

                def normalise_x1():
                    t = (s - 7) // 2
                    if not even and runs(t, i, TILES, 2):
                        upto(act, shift2_ready, t + 1, i, 2)
                        nc.scalar.activation(z[:, t % 2, :], x1_of(t, i), ACT.Identity,
                                             scale=rstd[:, 2 + t % 2, :], bias=shift[:, 2 + t % 2, :]
                                             ).then_inc(z_ready, 1)

                def split_q():
                    t = (s + 4) // 2
                    if even and runs(t, i, TILES, 2):
                        upto(act, q_normed, t + 1, i, 2)
                        nc.scalar.copy(q_hi[:, t % 2, :], x_in[:, t % 2, :]).then_inc(q_hi_ready, 1)

                def save_v():
                    t = s // 2
                    if even and runs(t, i, TILES, 2):
                        upto(act, v_t_ready, t + 1, i, 2)
                        upto(act, pv_done, t - 1, i, 2)
                        nc.scalar.copy(v_t[:, t % 2, :, :], ps_small[:].rearrange("p (c r) -> p c r", c=CHUNKS)
                                       ).then_inc(v_t_saved, 1)

                def save_q8():
                    t = (s - 9) // 2
                    if not even and runs(t, i, TILES, 2):
                        upto(act, q8_t_ready, t + 1, i, 2)
                        nc.scalar.mul(q8_t[:, t % 2, :, :], ps_small.ap().bitcast(BF16)[:, 0:L].rearrange(
                            "p (c r) -> p c r", c=CHUNKS), FP16_GUARD).then_inc(q8_t_saved, 1)

                def exponentials(u):
                    if runs(s, i, STEPS, BODY):
                        upto(act, st_ready, UNITS * s + u + 1, i, UNITS * BODY)
                        t = s // 2
                        if u == 0:
                            upto(act, pv_done, t - 1, i, 2)
                        nc.scalar.activation(probs[:, t % 2, PAIR * (s % 2) + u // CHUNKS, u % CHUNKS, :],
                                             ps_st[u % 2][:], ACT.Exp, scale=SM_SCALE).then_inc(probs_ready, 1)

                save_attention()
                exponentials(0)
                exponentials(1)
                save_max_rows()
                normalise_x()
                normalise_x1()
                exponentials(2)
                exponentials(3)
                split_q()
                save_q8()
                exponentials(4)
                exponentials(5)
                save_v()
                save_sums()
                exponentials(6)
                exponentials(7)
                split_k()
                if s in (2, 3, 4, 5):
                    c = s - 2
                    act.wait_ge(w_rounded, c + 1)
                    nc.scalar.mul(w_nan[:, c, :], w_f[:, c, :], FP16_GUARD).then_inc(w_guarded, 1)
                if s in (-1, 0, 1, 2):
                    c = s + 1
                    act.wait_ge(w_loaded, DMA)
                    act.wait_ge(small_loaded, 5 * DMA)
                    nc.scalar.mul(w_f[:, c, :], w_f[:, c, :], scalars[:, 4:5]).then_inc(w_scaled, 1)
                if s == 0:
                    act.wait_ge(small_loaded, 5 * DMA)
                    nc.scalar.activation(gates[:], scalars[:, 0:2], ACT.Tanh).then_inc(gates_ready, 1)

            steps(act, step)

        @block.vector
        def _(dve):
            def gains():
                dve.wait_ge(small_loaded, 5 * DMA)
                nc.vector.reciprocal(recips[:], scalars[:, 3:5]).then_inc(gates_chain, 1)
                dve.wait_ge(gates_ready, 1)
                nc.vector.tensor_scalar(att_gain[:], gates[:, 0:1], scalars[:, 2:3], None, ALU.mult
                                        ).then_inc(gates_chain, 1)
                dve.wait_ge(gates_chain, 2)
                nc.vector.tensor_scalar(ffn_scale[:], gates[:, 1:2], recips[:, 0:1], recips[:, 1:2],
                                        ALU.mult, ALU.mult).then_inc(gates_chain, 1)
                dve.wait_ge(gates_chain, 3)
                nc.vector.tensor_scalar(ffn_scale[:], ffn_scale[:], 1.0 / FP16_GUARD, None, ALU.mult
                                        ).then_inc(gates_chain, 1)
                dve.wait_ge(gates_chain, 4)

            def round_weights(s, part):
                if s in (0, 1, 2, 3) and part == 0:
                    c = s
                    dve.wait_ge(w_scaled, c + 1)
                    nc.vector.tensor_scalar(w_magic[:, c, :].bitcast(U32), w_f[:, c, :].bitcast(U32),
                                            EXPONENT_BITS, None, ALU.bitwise_and).then_inc(w_exponent_ready, 1)
                if s in (0, 1, 2, 3) and part == 1:
                    c = s
                    dve.wait_ge(w_exponent_ready, c + 1)
                    nc.vector.tensor_scalar(w_magic[:, c, :], w_magic[:, c, :], ROUND_AT, ROUND_LEAST,
                                            ALU.mult, ALU.max).then_inc(w_magic_ready, 1)
                if s in (3, 4, 5, 6) and part == 1:
                    c = s - 3
                    dve.wait_ge(w_guarded, c + 1)
                    nc.vector.tensor_tensor(w_nan[:, c, :], w_nan[:, c, :], w_nan[:, c, :], ALU.subtract
                                            ).then_inc(w_nan_ready, 1)

            def step(s, i):
                even = s % 2 == 0

                def maximum(u):
                    n = s + 2
                    if runs(n, i, STEPS, BODY):
                        upto(dve, s_ready, UNITS * n + u + 1, i, UNITS * BODY)
                        if u == 0:
                            upto(dve, max_t_ready, n - 1, i, BODY)
                        nc.vector.tensor_reduce(neg_max[:, n % 2, u:u + 1], s_bank(s, u)[:], AX, ALU.max,
                                                negate=True).then_inc(maxed, 1)

                def sum_pair(j):
                    n = s - 1
                    if runs(n, i, STEPS, BODY):
                        t = n // 2
                        upto(dve, probs_ready, UNITS * n + CHUNKS * j + 2, i, UNITS * BODY)
                        upto(dve, pv_done, t - 1, i, 2)
                        h = PAIR * (n % 2) + j
                        nc.vector.tensor_tensor(pair_sums[:, t % 2, h, :], probs[:, t % 2, h, 0, :],
                                                probs[:, t % 2, h, 1, :], ALU.add).then_inc(pairs_summed, 1)

                def low_halves_of_first():
                    dve.wait_ge(k_hi_ready, 1)
                    nc.vector.tensor_tensor(k_lo[:, 0, :], c_in[:, 0, :], k_hi[:, 0, :].bitcast(F32),
                                            ALU.subtract).then_inc(k_lo_ready, 1)
                    dve.wait_ge(q_hi_ready, 1)
                    nc.vector.tensor_tensor(q_lo[:, 0, :], x_in[:, 0, :], q_hi[:, 0, :].bitcast(F32),
                                            ALU.subtract).then_inc(q_lo_ready, 1)

                def measure_x():
                    t = (s + 5) // 2
                    if not even and runs(t, i, TILES, 2):
                        upto(dve, x_loaded[t % 2], DMA * (t // 2 + 1), i, DMA)
                        nc.vector.bn_stats(stats[:, t % 2, :], x_in[:, t % 2, :]).then_inc(stats_ready, 1)
                        upto(dve, stats_ready, t + 1, i, 2)

                def moments_of_x():
                    t = (s + 5) // 2
                    if not even and runs(t, i, TILES, 2):
                        nc.vector.bn_aggr(moments[:, t % 2, :], stats[:, t % 2, :]).then_inc(moments_ready, 1)

                def invert_sums():
                    t = (s - 5) // 2
                    if not even and runs(t, i, TILES, 2) and not is_last(t, i):
                        upto(dve, den_spread, DMA * (t + 1), i, 2 * DMA)
                        nc.vector.reciprocal(den_col[:, t % 2, :], den_col[:, t % 2, :]).then_inc(sums_inverted, 1)
                        upto(dve, sums_inverted, t + 1, i, 2)
                        nc.vector.tensor_scalar(den_col[:, t % 2, :], den_col[:, t % 2, :], att_gain[:], None,
                                                ALU.mult).then_inc(inv_ready, 1)

                def invert_last():
                    dve.wait_ge(o_normed, LAST - 1)
                    dve.wait_ge(den_saved, LAST + 1)
                    nc.vector.reciprocal(inv_sb[:, LAST % 2, :], den_sb[:]).then_inc(last_inverted, 1)

                def finish_last():
                    o, last_x1 = o_sb[:, LAST % 2, :], x1_of(LAST, None)
                    dve.wait_ge(last_inverted, 1)
                    dve.wait_ge(o_saved, LAST + 1)
                    nc.vector.scalar_tensor_tensor(out=o, in0=o, scalar=att_gain[:], in1=inv_sb[:, LAST % 2, :],
                                                   op0=ALU.mult, op1=ALU.mult).then_inc(last_normed, 1)
                    dve.wait_ge(last_normed, 1)
                    dve.wait_ge(res_loaded[LAST % 2], DMA * (LAST // 2 + 1))
                    nc.vector.tensor_tensor(last_x1, o, x_res[:, LAST % 2, :], ALU.add).then_inc(x1_ready, 1)
                    dve.wait_ge(x1_ready, LAST + 1)
                    nc.vector.bn_stats(stats[:, 2 + LAST % 2, :], last_x1).then_inc(stats2_ready, 1)
                    dve.wait_ge(stats2_ready, LAST + 1)
                    nc.vector.bn_aggr(moments[:, 2 + LAST % 2, :], stats[:, 2 + LAST % 2, :]
                                      ).then_inc(moments2_ready, 1)

                def round_to_float8():
                    t = (s - 7) // 2
                    if not even and runs(t, i, TILES, 2) and rounded_by_dve(t, i):
                        m, zz = magic[:, t % 2, :], z[:, t % 2, :]
                        dve.wait_ge(magic_ready, t + 1)
                        nc.vector.tensor_tensor(zz, zz, m, ALU.add).then_inc(rounded_up, 1)
                        dve.wait_ge(rounded_up, t + 1)
                        dve.wait_ge(q8_t_ready, t - 1)
                        nc.vector.tensor_tensor(q8[:, t % 2, :], zz, m, ALU.subtract).then_inc(q8_ready, 1)

                def measure_x1():
                    t = (s - 6) // 2
                    if even and runs(t, i, TILES, 2) and not is_last(t, i):
                        upto(dve, x1_ready, t + 1, i, 2)
                        nc.vector.bn_stats(stats[:, 2 + t % 2, :], x1_of(t, i)).then_inc(stats2_ready, 1)
                        upto(dve, stats2_ready, t + 1, i, 2)

                def moments_of_x1():
                    t = (s - 6) // 2
                    if even and runs(t, i, TILES, 2) and not is_last(t, i):
                        nc.vector.bn_aggr(moments[:, 2 + t % 2, :], stats[:, 2 + t % 2, :]
                                          ).then_inc(moments2_ready, 1)

                def powers_of_two():
                    t = (s - 7) // 2
                    if not even and runs(t, i, TILES, 2):
                        upto(dve, z_ready, t + 1, i, 2)
                        nc.vector.tensor_scalar(magic[:, t % 2, :].bitcast(U32), z[:, t % 2, :].bitcast(U32),
                                                EXPONENT_BITS, None, ALU.bitwise_and).then_inc(exponent_ready, 1)

                def magic_numbers():
                    t = (s - 7) // 2
                    if not even and runs(t, i, TILES, 2):
                        upto(dve, exponent_ready, t + 1, i, 2)
                        nc.vector.tensor_scalar(magic[:, t % 2, :], magic[:, t % 2, :], ROUND_AT, ROUND_LEAST,
                                                ALU.mult, ALU.max).then_inc(magic_ready, 1)

                def gain_of_rows():
                    t = (s - 9) // 2
                    if not even and runs(t, i, TILES, 2):
                        upto(dve, nan_ready, t + 1, i, 2)
                        nc.vector.tensor_scalar(ffn_gain[:, t % 2, :], ps_small[:, 0:1], ffn_scale[:], None,
                                                ALU.add).then_inc(gain_ready, 1)

                def add_product():
                    t = (s - 10) // 2
                    if even and runs(t, i, TILES, 2):
                        upto(dve, y_ready, t + 1, i, 2)
                        upto(dve, gain_ready, t + 1, i, 2)
                        upto(dve, y_sb_free[t % 2], DMA * (t // 2 + 1), i, DMA)
                        nc.vector.scalar_tensor_tensor(out=y_sb[:, t % 2, :], in0=ps_y[:], scalar=ffn_gain[:, t % 2, :],
                                                       in1=x1_of(t, i), op0=ALU.mult,
                                                       op1=ALU.add).then_inc(y_added, 1)

                if s == -4:
                    low_halves_of_first()
                maximum(0)
                maximum(1)
                add_product()
                if s == STEPS + 3:
                    finish_last()
                invert_sums()
                if not even:
                    sum_pair(0)
                maximum(2)
                maximum(3)
                if even:
                    sum_pair(0)
                round_weights(s, 0)
                powers_of_two()
                maximum(4)
                maximum(5)
                measure_x1()
                round_weights(s, 1)
                magic_numbers()
                measure_x()
                maximum(6)
                moments_of_x1()
                moments_of_x()
                maximum(7)
                gain_of_rows()
                sum_pair(1)
                if s == STEPS + 1:
                    invert_last()
                round_to_float8()
                if s == -2:
                    dve.wait_ge(constants_ready, CONSTANTS)
                    nc.vector.tensor_copy(ident16[:], ident[:]).then_inc(ident16_ready, 1)
                if s == 1:
                    gains()

            steps(dve, step)

        @block.tensor
        def _(pe):
            pe.wait_ge(constants_ready, CONSTANTS)

            def step(s, i):
                even = s % 2 == 0

                def scores_t(u):
                    if runs(s, i, STEPS, BODY):
                        slot, c = PAIR * (s % BODY) + u // CHUNKS, u % CHUNKS
                        if s == 0 and u == 0:
                            pe.wait_ge(ones_row_ready, 1)
                        if u == 0:
                            upto(pe, max_stacked[s % BODY], DMA * (s // BODY + 1), i, DMA)
                        upto(pe, probs_ready, UNITS * s + u - 1, i, UNITS * BODY)
                        nc.tensor.matmul(ps_st[u % 2][:], k_stack[0:ONES_ROW + 1, slot, c * P:(c + 1) * P],
                                         q_stack[0:ONES_ROW + 1, slot, :], start=True, stop=True
                                         ).then_inc(st_ready, 1)

                def scores(u):
                    n = s + 2
                    if runs(n, i, STEPS, BODY):
                        slot, c = PAIR * (n % BODY) + u // CHUNKS, u % CHUNKS
                        if c == 0:
                            upto(pe, stacked[slot], DMA * STACK_DMAS * (n // BODY + 1), i, DMA * STACK_DMAS)
                        upto(pe, maxed, UNITS * n + u + 1 - (4 if s < 0 else 2), i, UNITS * BODY)
                        nc.tensor.matmul(s_bank(s, u)[:], q_stack[0:ONES_ROW, slot, c * P:(c + 1) * P],
                                         k_stack[0:ONES_ROW, slot, :], start=True, stop=True).then_inc(s_ready, 1)

                def attend(g):
                    t = (s - 2) // 2
                    if not runs(t, i, TILES, 2):
                        return

                    def weigh(c):
                        for h in range(HEADS_PER_TILE):
                            rows = slice(D * h, D * h + D)
                            last = nc.tensor.matmul(ps_o[rows, :], v_t[:, t % 2, c, rows],
                                                    probs[:, t % 2, h, c, :], start=c == 0, stop=c == CHUNKS - 1)
                        return last

                    def add_up(moving, start, stop):
                        for h in range(HEADS_PER_TILE):
                            last = nc.tensor.matmul(ps_den[D * h:D * h + D, :], ones[:], moving[:, h, :],
                                                    start=start, stop=stop)
                        return last

                    if even and g == 0:
                        upto(pe, probs_ready, 2 * UNITS * (t + 1) - CHUNKS + 1, i, 4 * UNITS)
                        upto(pe, v_t_saved, t + 1, i, 2)
                        upto(pe, o_saved, t, i, 2)
                        weigh(0)
                    elif even and g == 1:
                        upto(pe, probs_ready, 2 * UNITS * (t + 1) - CHUNKS + 2, i, 4 * UNITS)
                        weigh(1)
                    elif even and g == 2:
                        upto(pe, probs_ready, 2 * UNITS * (t + 1) - CHUNKS + 3, i, 4 * UNITS)
                        upto(pe, den_saved, t, i, 2)
                        add_up(probs[:, t % 2, :, 2, :], True, False)
                    elif even and g == 3:
                        upto(pe, probs_ready, 2 * UNITS * (t + 1), i, 4 * UNITS)
                        add_up(probs[:, t % 2, :, 3, :], False, False)
                    elif g == 0:
                        weigh(2)
                    elif g == 1:
                        upto(pe, pairs_summed, HEADS_PER_TILE * (t + 1), i, 2 * HEADS_PER_TILE)
                        add_up(pair_sums[:, t % 2, :, :], False, True).then_inc(sums_done, 1)
                    elif g == 3:
                        weigh(3).then_inc(pv_done, 1)

                def transpose_max():
                    n = s + 1
                    if runs(n, i, STEPS, BODY):
                        upto(pe, maxed, UNITS * (n + 1), i, UNITS * BODY)
                        upto(pe, max_rows_ready, n, i, BODY)
                        if even:
                            upto(pe, gain_ready, (s - 10) // 2 + 1, i, 2)
                        else:
                            upto(pe, v_t_saved, (s - 1) // 2 + 1, i, 2)
                        nc.tensor.transpose(ps_small[0:UNITS, 0:P], neg_max[:, n % 2, :], ident[:]
                                            ).then_inc(max_t_ready, 1)

                def transpose_v():
                    t = s // 2
                    if even and runs(t, i, TILES, 2):
                        upto(pe, v_loaded, DMA * (t + 1), i, 2 * DMA)
                        upto(pe, max_rows_ready, s + 2, i, BODY)
                        for c in range(CHUNKS):
                            last = nc.tensor.transpose(ps_small[:, c * P:(c + 1) * P],
                                                       v_in[:, c * P:(c + 1) * P], ident[:])
                        last.then_inc(v_t_ready, 1)

                def transpose_q8():
                    t = (s - 9) // 2
                    if not even and runs(t, i, TILES, 2):
                        upto(pe, q8_ready, t + 1, i, 2)
                        upto(pe, max_rows_ready, min(s + 2, STEPS) if i is None else s + 2, i, BODY)
                        upto(pe, v_t_saved, min((s - 1) // 2 + 1, TILES) if i is None else (s - 1) // 2 + 1, i, 2)
                        upto(pe, gain_ready, t, i, 2)
                        if t == 0:
                            pe.wait_ge(ident16_ready, 1)
                        for c in range(CHUNKS):
                            last = nc.tensor.transpose(ps_small.ap().bitcast(BF16)[:, c * P:(c + 1) * P],
                                                       q8[:, t % 2, c * P:(c + 1) * P], ident16[:])
                        last.then_inc(q8_t_ready, 1)

                def product():
                    t = (s - 9) // 2
                    if not even and runs(t, i, TILES, 2):
                        upto(pe, q8_t_saved, t + 1, i, 2)
                        upto(pe, y_added, t, i, 2)
                        if t == 0:
                            pe.wait_ge(weights_ready, CHUNKS)
                        for c in range(CHUNKS):
                            last = nc.tensor.matmul(ps_small[:, 0:1], q8_t[:, t % 2, c, :], zero16[:],
                                                    start=c == 0, stop=c == CHUNKS - 1)
                        last.then_inc(nan_ready, 1)
                        for c in range(CHUNKS):
                            last = nc.tensor.matmul(ps_y[:], q8_t[:, t % 2, c, :], w8[:, c, :],
                                                    start=c == 0, stop=c == CHUNKS - 1)
                        last.then_inc(y_ready, 1)

                for u in range(UNITS):
                    scores_t(u)
                    scores(u)
                    if u % 2 == 1:
                        attend(u // 2)
                    if u == 1:
                        transpose_max()
                    if u == 3:
                        transpose_v()
                        transpose_q8()
                    if u == 5:
                        product()

            steps(pe, step)


_INS = ["x", "ctx_2048", "g_xattn", "g_ffn", "L0_xattn_gamma", "L0_ffn_input2", "L0_ffn_scale", "L0_ffn_scale1"]


def kernel(**inputs):
    import numpy as _np
    import concourse.bacc as _bacc
    from concourse import mybir as _mybir
    from concourse.bass_utils import run_bass_kernel_spmd as _run

    nc = _bacc.Bacc("TRN2", target_bir_lowering=False, num_devices=1)
    arrays, args = {}, []
    for name in _INS:
        a = _np.ascontiguousarray(inputs[name])
        arrays[f"in_{name}"] = a
        args.append(nc.dram_tensor(f"in_{name}", a.shape, _mybir.dt.from_np(a.dtype), kind="ExternalInput").ap())
    args.append(nc.dram_tensor("out_x", (IMAGES, CHANNELS, L), F32, kind="ExternalOutput").ap())
    build(nc, *args)
    r = _run(nc, [arrays], core_ids=[0])
    return r.results[0]["out_x"]
```
